# Optimizing a Trainium2 kernel written in Bass

```python
import numpy as np
import jax
import jax.numpy as jnp

def _softmax(x, axis=-1):
    return jax.nn.softmax(x, axis=axis)

def _gelu(x):
    return jax.nn.gelu(x, approximate=True)

def _silu(x):
    return jax.nn.silu(x)

def _sigmoid(x):
    return jax.nn.sigmoid(x)

def _layernorm(x, axis=-1, eps=1e-05):
    m = jnp.mean(x, axis=axis, keepdims=True)
    v = jnp.var(x, axis=axis, keepdims=True)
    return (x - m) / jnp.sqrt(v + eps)

def _scatter_add(tgt, idx, src, axis=0):
    return tgt.at[idx].add(src)

def _segment_sum(src, seg, n):
    return jax.ops.segment_sum(src, seg, n)
kernel_name = 'mk_xattn_seq_d2_seqx_r4_5b8fab'

def setup_inputs(seed: int=0):
    np.random.seed(seed)
    _w = jnp.asarray

    def _rec_inputs():
        import jax
        import jax.numpy as jnp
        _rk = jax.random.key(seed)
        x = -0.0002928 + 1 * jax.random.normal(jax.random.fold_in(_rk, 1), (64, 128, 512), jnp.float32)
        _lenS = 128 - jax.random.randint(jax.random.fold_in(_rk, 7), (64,), 0, max(1, 128 // 4) + 1, jnp.int32)
        _lenS2 = 128 - jax.random.randint(jax.random.fold_in(_rk, 8), (64,), 0, max(1, 128 // 4) + 1, jnp.int32)
        _ctx_2048P = jax.random.normal(jax.random.fold_in(_rk, 11), (64, 16, 512), jnp.float32)
        _ctx_2048c = jax.random.dirichlet(jax.random.fold_in(_rk, 511), 0.3 * jnp.ones((16,), jnp.float32), (64, 128))
        _ctx_2048t = jnp.einsum('bsk,bkd->bsd', _ctx_2048c, _ctx_2048P)
        _ctx_2048t = _ctx_2048t * jax.lax.rsqrt(jnp.mean(jnp.square(_ctx_2048t)) + 1e-12) * 0.953939
        ctx_2048 = -1.39393e-06 + 0.999914 * (_ctx_2048t + 0.3 * jax.random.normal(jax.random.fold_in(_rk, 611), (64, 128, 512), jnp.float32))
        _validS = jnp.arange(128)[None, :] < _lenS[:, None]
        _validS2 = jnp.arange(128)[None, :] < _lenS2[:, None]
        _causal = jnp.tril(jnp.ones((128, 128), dtype=bool))
        mask_BxS2_bf1 = jnp.ones((64, 128), dtype=bool)
        return (x, ctx_2048, mask_BxS2_bf1)
    x, ctx_2048, mask_BxS2_bf1 = _rec_inputs()

    def _L0_xattn_setup():
        import jax, jax.numpy as jnp
        import numpy as np
        EPS = 1e-05

        def _inorm(x):
            m = jnp.mean(x, axis=-1, keepdims=True)
            v = jnp.var(x, axis=-1, keepdims=True)
            return (x - m) * jax.lax.rsqrt(v + EPS)

        def _conv1x1(W, b, x):
            return jnp.einsum('oc,bct->bot', W, x) + b[None, :, None]
        key = jax.random.key(seed)
        ks = jax.random.split(key, 10)
        B, C, T = (4, 128, 512)
        s = 1.0 / np.sqrt(C)
        return {'x_c': jax.random.normal(ks[0], (B, C, T), jnp.float32), 'x_s': jax.random.normal(ks[1], (B, C, T), jnp.float32), 'Wn': jax.random.normal(ks[2], (C, C), jnp.float32) * s, 'bn': jax.random.normal(ks[3], (C,), jnp.float32) * s, 'Wm': jax.random.normal(ks[4], (C, C), jnp.float32) * s, 'bm': jax.random.normal(ks[5], (C,), jnp.float32) * s, 'Wl': jax.random.normal(ks[6], (C, C), jnp.float32) * s, 'bl': jax.random.normal(ks[7], (C,), jnp.float32) * s, 'Wo': jax.random.normal(ks[8], (C, C), jnp.float32) * s, 'bo': jax.random.normal(ks[9], (C,), jnp.float32) * s}
    _L0_xattn_all = _L0_xattn_setup()
    _L0_xattn_in = {k: v for k, v in _L0_xattn_all.items() if k in ('Wn', 'bn', 'Wm', 'bm', 'Wl', 'bl', 'Wo', 'bo')}
    del _L0_xattn_all

    def _L1_xattn_setup():
        import jax, jax.numpy as jnp
        import numpy as np
        D = 512
        H = 16
        HD = D // H
        INNER = 4 * D
        EPS = 1e-05

        def layer_norm(x, w, b):
            mu = jnp.mean(x, axis=-1, keepdims=True)
            var = jnp.mean(jnp.square(x - mu), axis=-1, keepdims=True)
            return (x - mu) * jax.lax.rsqrt(var + EPS) * w + b
        key = jax.random.key(seed)
        ks = jax.random.split(key, 12)
        B, LQ, LK = (4, 256, 512)
        std = 0.02
        inp = {'hidden_states': jax.random.normal(ks[0], (B, LQ, D), jnp.float32), 'encoder_hidden_states': jax.random.normal(ks[1], (B, LK, D), jnp.float32), 'encoder_attention_mask': jnp.ones((B, LK), dtype=bool), 'ln1_w': jnp.ones((D,), jnp.float32), 'ln1_b': jnp.zeros((D,), jnp.float32), 'q_w': jax.random.normal(ks[2], (D, D), jnp.float32) * std, 'q_b': jnp.zeros((D,), jnp.float32), 'k_w': jax.random.normal(ks[3], (D, D), jnp.float32) * std, 'k_b': jnp.zeros((D,), jnp.float32), 'v_w': jax.random.normal(ks[4], (D, D), jnp.float32) * std, 'v_b': jnp.zeros((D,), jnp.float32), 'cproj_w': jax.random.normal(ks[5], (D, D), jnp.float32) * std, 'cproj_b': jnp.zeros((D,), jnp.float32), 'ln2_w': jnp.ones((D,), jnp.float32), 'ln2_b': jnp.zeros((D,), jnp.float32), 'fc_w': jax.random.normal(ks[6], (D, INNER), jnp.float32) * std, 'fc_b': jnp.zeros((INNER,), jnp.float32), 'proj_w': jax.random.normal(ks[7], (INNER, D), jnp.float32) * std, 'proj_b': jnp.zeros((D,), jnp.float32)}
        return inp
    _L1_xattn_all = _L1_xattn_setup()
    _L1_xattn_in = {k: v for k, v in _L1_xattn_all.items() if k in ('ln1_w', 'ln1_b', 'q_w', 'q_b', 'k_w', 'k_b', 'v_w', 'v_b', 'cproj_w', 'cproj_b', 'ln2_w', 'ln2_b', 'fc_w', 'fc_b', 'proj_w', 'proj_b')}
    del _L1_xattn_all
    return {'x': x, 'ctx_2048': ctx_2048, 'mask_BxS2_bf1': mask_BxS2_bf1, 'L0_xattn_Wn': _L0_xattn_in['Wn'], 'L0_xattn_bn': _L0_xattn_in['bn'], 'L0_xattn_Wm': _L0_xattn_in['Wm'], 'L0_xattn_bm': _L0_xattn_in['bm'], 'L0_xattn_Wl': _L0_xattn_in['Wl'], 'L0_xattn_bl': _L0_xattn_in['bl'], 'L0_xattn_Wo': _L0_xattn_in['Wo'], 'L0_xattn_bo': _L0_xattn_in['bo'], 'L1_xattn_ln1_w': _L1_xattn_in['ln1_w'], 'L1_xattn_ln1_b': _L1_xattn_in['ln1_b'], 'L1_xattn_q_w': _L1_xattn_in['q_w'], 'L1_xattn_q_b': _L1_xattn_in['q_b'], 'L1_xattn_k_w': _L1_xattn_in['k_w'], 'L1_xattn_k_b': _L1_xattn_in['k_b'], 'L1_xattn_v_w': _L1_xattn_in['v_w'], 'L1_xattn_v_b': _L1_xattn_in['v_b'], 'L1_xattn_cproj_w': _L1_xattn_in['cproj_w'], 'L1_xattn_cproj_b': _L1_xattn_in['cproj_b'], 'L1_xattn_ln2_w': _L1_xattn_in['ln2_w'], 'L1_xattn_ln2_b': _L1_xattn_in['ln2_b'], 'L1_xattn_fc_w': _L1_xattn_in['fc_w'], 'L1_xattn_fc_b': _L1_xattn_in['fc_b'], 'L1_xattn_proj_w': _L1_xattn_in['proj_w'], 'L1_xattn_proj_b': _L1_xattn_in['proj_b']}

def reference(x, ctx_2048, mask_BxS2_bf1, L0_xattn_Wn, L0_xattn_bn, L0_xattn_Wm, L0_xattn_bm, L0_xattn_Wl, L0_xattn_bl, L0_xattn_Wo, L0_xattn_bo, L1_xattn_ln1_w, L1_xattn_ln1_b, L1_xattn_q_w, L1_xattn_q_b, L1_xattn_k_w, L1_xattn_k_b, L1_xattn_v_w, L1_xattn_v_b, L1_xattn_cproj_w, L1_xattn_cproj_b, L1_xattn_ln2_w, L1_xattn_ln2_b, L1_xattn_fc_w, L1_xattn_fc_b, L1_xattn_proj_w, L1_xattn_proj_b):
    import jax
    import jax.numpy as jnp

    def _L0_xattn_ref(x_c, x_s, Wn, bn, Wm, bm, Wl, bl, Wo, bo):
        import jax, jax.numpy as jnp
        import numpy as np
        EPS = 1e-05

        def _inorm(x):
            m = jnp.mean(x, axis=-1, keepdims=True)
            v = jnp.var(x, axis=-1, keepdims=True)
            return (x - m) * jax.lax.rsqrt(v + EPS)

        def _conv1x1(W, b, x):
            return jnp.einsum('oc,bct->bot', W, x) + b[None, :, None]
        Mn = _conv1x1(Wn, bn, _inorm(x_c))
        Mm = _conv1x1(Wm, bm, _inorm(x_s))
        A = jax.nn.softmax(jnp.einsum('bct,bcs->bts', Mn, Mm), axis=-1)
        Ml = _conv1x1(Wl, bl, x_s)
        Mo = jnp.einsum('bcs,bts->bct', Ml, A)
        return _conv1x1(Wo, bo, Mo) + x_c

    def _L1_xattn_ref(hidden_states, encoder_hidden_states, encoder_attention_mask, ln1_w, ln1_b, q_w, q_b, k_w, k_b, v_w, v_b, cproj_w, cproj_b, ln2_w, ln2_b, fc_w, fc_b, proj_w, proj_b):
        import jax, jax.numpy as jnp
        import numpy as np
        D = 512
        H = 16
        HD = D // H
        INNER = 4 * D
        EPS = 1e-05

        def layer_norm(x, w, b):
            mu = jnp.mean(x, axis=-1, keepdims=True)
            var = jnp.mean(jnp.square(x - mu), axis=-1, keepdims=True)
            return (x - mu) * jax.lax.rsqrt(var + EPS) * w + b
        B, LQ, _ = hidden_states.shape
        LK = encoder_hidden_states.shape[1]
        residual = hidden_states
        x = layer_norm(hidden_states, ln1_w, ln1_b)
        q = (x @ q_w + q_b).reshape(B, LQ, H, HD).transpose(0, 2, 1, 3)
        k = (encoder_hidden_states @ k_w + k_b).reshape(B, LK, H, HD).transpose(0, 2, 1, 3)
        v = (encoder_hidden_states @ v_w + v_b).reshape(B, LK, H, HD).transpose(0, 2, 1, 3)
        scale = 1.0 / np.sqrt(HD).astype(np.float32)
        scores = jnp.einsum('bhqd,bhkd->bhqk', q, k) * scale
        mask = encoder_attention_mask[:, None, None, :]
        mask_value = jnp.finfo(scores.dtype).min
        scores = jnp.where(mask, scores, mask_value)
        attn = jax.nn.softmax(scores, axis=-1)
        out = jnp.einsum('bhqk,bhkd->bhqd', attn, v)
        out = out.transpose(0, 2, 1, 3).reshape(B, LQ, D)
        out = out @ cproj_w + cproj_b
        hidden = out + residual
        residual = hidden
        y = layer_norm(hidden, ln2_w, ln2_b)
        y = jax.nn.gelu(y @ fc_w + fc_b, approximate=True)
        y = y @ proj_w + proj_b
        return residual + y
    x = _L0_xattn_ref(x, ctx_2048, L0_xattn_Wn, L0_xattn_bn, L0_xattn_Wm, L0_xattn_bm, L0_xattn_Wl, L0_xattn_bl, L0_xattn_Wo, L0_xattn_bo)
    x = _L1_xattn_ref(x, ctx_2048, mask_BxS2_bf1, L1_xattn_ln1_w, L1_xattn_ln1_b, L1_xattn_q_w, L1_xattn_q_b, L1_xattn_k_w, L1_xattn_k_b, L1_xattn_v_w, L1_xattn_v_b, L1_xattn_cproj_w, L1_xattn_cproj_b, L1_xattn_ln2_w, L1_xattn_ln2_b, L1_xattn_fc_w, L1_xattn_fc_b, L1_xattn_proj_w, L1_xattn_proj_b)
    return x

_drawn_inputs = setup_inputs


def setup_inputs(seed=0):
    import zlib

    import numpy as np

    out = dict(_drawn_inputs(seed))
    spreads = {'L1_xattn_ln1_w': (1.0, 0.6),
     'L1_xattn_ln1_b': (0.0, 0.8),
     'L1_xattn_q_b': (0.0, 0.8),
     'L1_xattn_k_b': (0.0, 0.8),
     'L1_xattn_v_b': (0.0, 0.295),
     'L1_xattn_cproj_b': (0.0, 0.1),
     'L1_xattn_ln2_w': (1.0, 0.568),
     'L1_xattn_ln2_b': (0.0, 0.532),
     'L1_xattn_fc_b': (0.0, 0.1),
     'L1_xattn_proj_b': (0.0, 0.1)}
    factors = {'L0_xattn_bm': 8.0, 'L1_xattn_q_w': 8.0, 'L1_xattn_k_w': 8.0}
    for name, (base, spread) in spreads.items():
        noise = np.random.default_rng([zlib.crc32(name.encode()), seed]).standard_normal(out[name].shape)
        drawn = base * np.exp(spread * noise) if base else spread * noise
        out[name] = jnp.asarray(drawn.astype(out[name].dtype))
    for name, factor in factors.items():
        out[name] = (out[name] * factor).astype(out[name].dtype)
    return out
```

```python
from contextlib import ExitStack

import concourse.bass as bass
from concourse import mybir

F32 = mybir.dt.float32
F32R = mybir.dt.float32r
BF16 = mybir.dt.bfloat16
U8 = mybir.dt.uint8
ALU = mybir.AluOpType
ACT = mybir.ActivationFunctionType
AX_X = mybir.AxisListType.X

P = 128
EPS = 1e-5
HEADS = 16
MASKED = 3.3895313892515355e38


class Item:

    def __init__(self, pair, offset, count):
        self.pair, self.offset, self.count = pair, offset, count

    def __add__(self, k):
        return Item(self.pair, self.offset + k, self.count)

    def exists(self):
        return not isinstance(self.pair, int) or 0 <= self.offset < self.count

    def has_before(self, k=1):
        return not isinstance(self.pair, int) or self.offset - k >= 0

    @property
    def parity(self):
        return self.offset % 2

    @property
    def number(self):
        return self.pair * 2 + self.offset

    def nth(self, per_item, k):
        return self.pair * (2 * per_item) + (self.offset * per_item + k)

    def dma(self, k=1):
        return self.pair * (16 * k) + (self.offset // 2 + 1) * (16 * k)


def attention_pass(nc, x, ctx, mask, w, hidden):
    B, C, T = x.shape
    D = T
    DC = D // P
    HD = D // HEADS
    HV = HD + 1
    SCALE = float(HD) ** -0.5
    assert C == P and D == 4 * P and HD == 32

    with ExitStack() as stack:
        def sb(name, shape, dt=F32):
            return stack.enter_context(nc.sbuf_tensor(name, shape, dt))

        def sem(name):
            return stack.enter_context(nc.semaphore(name))

        bank = [stack.enter_context(nc.psum_tensor(f"bank{i}", [P, 512], F32)) for i in range(8)]

        qkvc_hi = sb("qkvc_hi", [P, 4, DC, D], F32R)
        qkvc_lo = sb("qkvc_lo", [P, 4, DC, D], F32R)
        stage = sb("stage", [P, 2, DC, D])
        small = sb("small", [P, 4, P])
        small_t = sb("small_t", [P, 4, P])
        vecs = sb("vecs", [P, 5, DC])
        bias0 = sb("bias0", [P, 4])
        out0_bias = sb("out0_bias", [P, 1])
        q_bias = sb("q_bias", [P, DC])
        vb_wide = sb("vb_wide", [P, DC, P])
        cb_row = sb("cb_row", [1, D])
        attn_bias = sb("attn_bias", [P, D])
        ident = sb("ident", [P, P])
        ones = sb("ones", [P, P])
        masked_bf = sb("masked_bf", [P, P], BF16)
        eps_t = sb("eps_t", [P, 2])
        neghalf = sb("neghalf", [P, 2])

        x_in = sb("x_in", [P, 2, T])
        ctx_in = sb("ctx_in", [P, 2, T])
        in_stats = sb("in_stats", [P, 2, 6])
        in_mv = sb("in_mv", [P, 2, 2])
        in_ve = sb("in_ve", [P, 2])
        in_rstd = sb("in_rstd", [P, 2])
        xn = sb("xn", [P, T])
        cn = sb("cn", [P, T])
        mn_hi = sb("mn_hi", [P, T], F32R)
        mn_lo = sb("mn_lo", [P, T], F32R)
        mm_hi = sb("mm_hi", [P, T], F32R)
        mm_lo = sb("mm_lo", [P, T], F32R)
        ctxT_hi = sb("ctxT_hi", [P, DC, P], F32R)
        ctxT_lo = sb("ctxT_lo", [P, DC, P], F32R)
        negmax0 = sb("negmax0", [P, DC])
        sum0 = sb("sum0", [P, DC])
        rsum0 = sb("rsum0", [P, DC])
        A = sb("A", [P, DC, T])
        at_hi = sb("at_hi", [P, DC, T], F32R)
        at_lo = sb("at_lo", [P, DC, T], F32R)
        u_sb = sb("u_sb", [P, T])
        x1 = sb("x1", [P, D])
        x1_stats = sb("x1_stats", [P, 6])
        x1_mv = sb("x1_mv", [P, 2])
        x1_ve = sb("x1_ve", [P, 1])
        x1_rstd = sb("x1_rstd", [P, 1])
        x1b = sb("x1b", [P, 2, D])
        x1n = sb("x1n", [P, D])
        xnT_hi = sb("xnT_hi", [P, DC, P], F32R)
        xnT_lo = sb("xnT_lo", [P, DC, P], F32R)
        q_sb = sb("q_sb", [P, D])
        k_sb = sb("k_sb", [P, D])
        qT = sb("qT", [P, DC, P])
        kT = sb("kT", [P, DC, P])
        v_sb = sb("v_sb", [P, 2, HEADS, HV])
        mask_u8 = sb("mask_u8", [P, 2, P], U8)
        mask_less_1 = sb("mask_less_1", [P, P], BF16)
        rowmax1 = sb("rowmax1", [P, 4, 4])
        probs = sb("probs", [P, 4, 4, P])
        pT = sb("pT", [P, 4, 4, P])
        rsum1 = sb("rsum1", [P, HEADS])
        attn = sb("attn", [P, HEADS, HD])
        outT_hi = sb("outT_hi", [P, DC, P], F32R)
        outT_lo = sb("outT_lo", [P, DC, P], F32R)
        hid = sb("hid", [P, 2, D])

        sp_steps = sem("sp_steps")
        small_in = sem("small_in")
        stage_in = [sem(f"stage_in{i}") for i in range(2)]
        consts_set = sem("consts_set")
        ident_zero = sem("ident_zero")
        ident_set = sem("ident_set")
        vb_wide_set = sem("vb_wide_set")
        small_turned = sem("small_turned")
        small_copied = sem("small_copied")
        wow_done = sem("wow_done")
        wow_copied = sem("wow_copied")
        q_bias_done = sem("q_bias_done")
        attn_bias_done = sem("attn_bias_done")
        biases_set = sem("biases_set")
        w_hi_set = sem("w_hi_set")
        w_lo_set = sem("w_lo_set")
        x_loaded = [sem(f"x_loaded{i}") for i in range(2)]
        ctx_loaded = [sem(f"ctx_loaded{i}") for i in range(2)]
        mask_loaded = [sem(f"mask_loaded{i}") for i in range(2)]
        hid_stored = [sem(f"hid_stored{i}") for i in range(2)]
        in_stat = sem("in_stat")
        stats_seen = sem("stats_seen")
        in_aggr = sem("in_aggr")
        in_veps = sem("in_veps")
        in_rstd_ready = sem("in_rstd_ready")
        xn_ready = sem("xn_ready")
        ctxT_turned = sem("ctxT_turned")
        ctxT_hi_set = sem("ctxT_hi_set")
        ctxT_lo_set = sem("ctxT_lo_set")
        m_done = sem("m_done")
        m_hi_set = sem("m_hi_set")
        m_lo_set = sem("m_lo_set")
        s0_done = sem("s0_done")
        max0_set = sem("max0_set")
        exp0_done = sem("exp0_done")
        rsum0_set = sem("rsum0_set")
        a_scaled = sem("a_scaled")
        at_turned = sem("at_turned")
        at_hi_set = sem("at_hi_set")
        at_lo_set = sem("at_lo_set")
        u_done = sem("u_done")
        u_copied = sem("u_copied")
        out0_done = sem("out0_done")
        x1_set = sem("x1_set")
        x1_stat = sem("x1_stat")
        x1_aggr = sem("x1_aggr")
        x1_veps = sem("x1_veps")
        x1_rstd_ready = sem("x1_rstd_ready")
        x1n_set = sem("x1n_set")
        x1b_set = sem("x1b_set")
        xnT_turned = sem("xnT_turned")
        xnT_hi_set = sem("xnT_hi_set")
        xnT_lo_set = sem("xnT_lo_set")
        q_done = sem("q_done")
        q_copied = sem("q_copied")
        qT_turned = sem("qT_turned")
        qT_set = sem("qT_set")
        k_done = sem("k_done")
        k_copied = sem("k_copied")
        kT_turned = sem("kT_turned")
        kT_set = sem("kT_set")
        v_done = sem("v_done")
        v_copied = sem("v_copied")
        mask_set = sem("mask_set")
        s1_done = sem("s1_done")
        max1_set = sem("max1_set")
        shifted = sem("shifted")
        exp1_done = sem("exp1_done")
        pT_turned = sem("pT_turned")
        pT_copied = sem("pT_copied")
        pv_done = sem("pv_done")
        rsum1_set = sem("rsum1_set")
        attn_set = sem("attn_set")
        outT_turned = sem("outT_turned")
        outT_hi_set = sem("outT_hi_set")
        outT_lo_set = sem("outT_lo_set")
        cproj_done = sem("cproj_done")
        hid_set = sem("hid_set")

        SMALL_DMAS = 4 + 5 + 4 + 1
        WEIGHTS = ("k_w", "v_w", "q_w", "cproj_w")
        K_W, V_W, Q_W, C_W = range(4)

        FIRST, LOOPED, LAST = -1, 3, B + 1
        PAIRS = (B - 1 - LOOPED) // 2

        def slots(eng, slot):
            for s in range(FIRST, LOOPED):
                slot(Item(0, s, B))
            with eng.Fori(0, PAIRS) as pair:
                for s in range(LOOPED, LOOPED + 2):
                    slot(Item(pair, s, B))
            for s in range(LOOPED + 2 * PAIRS, LAST + 1):
                slot(Item(0, s, B))

        def three_passes(pe, out, a_hi, a_lo, b_hi, b_lo, first=True, last=True):
            pe.matmul(out, a_hi, b_lo, start=first, stop=False)
            pe.matmul(out, a_lo, b_hi, start=False, stop=False)
            return pe.matmul(out, a_hi, b_hi, start=False, stop=last)

        block = stack.enter_context(nc.Block())

        @block.sync
        def _(sp):
            def after(semaphore, value):
                sp.wait_ge(semaphore, value)
                sp.sem_inc(sp_steps, 1)

            for i, n in enumerate(("Wn", "Wm", "Wl", "Wo")):
                sp.dma_start(small[:, i, :], w[n]).then_inc(small_in, 16)
            for i, n in enumerate(("ln1_w", "ln1_b", "q_b", "k_b", "v_b")):
                sp.dma_start(vecs[:, i, :], w[n].rearrange("(c p) -> p c", p=P),
                             allow_slow_non_contiguous=True).then_inc(small_in, 16)
            for i, n in enumerate(("bn", "bm", "bl", "bo")):
                sp.dma_start(bias0[:, i:i + 1], w[n].rearrange("(p a) -> p a", a=1)).then_inc(small_in, 16)
            sp.dma_start(cb_row[:], w["cproj_b"].rearrange("(a d) -> a d", a=1)).then_inc(small_in, 16)

            def load(e):
                if e.has_before(2):
                    after(x1_set, (e + -2).nth(1, 1))
                    after(ctxT_turned, (e + -2).nth(1, 1))
                    after(xn_ready, (e + -2).nth(2, 2))
                u = e.parity
                sp.dma_start(x_in[:, u, :], x[e.number]).then_inc(x_loaded[u], 16)
                sp.dma_start(ctx_in[:, u, :], ctx[e.number]).then_inc(ctx_loaded[u], 16)

            def stage_weight(i):
                if i >= 2:
                    sp.wait_ge(w_hi_set, 4 * (i - 1))
                    sp.wait_ge(w_lo_set, 4 * (i - 1))
                sp.dma_start(stage[:, i % 2, :, :],
                             w[WEIGHTS[i]].rearrange("(c p) n -> p c n", p=P)).then_inc(stage_in[i % 2], 16)

            load(Item(0, 0, B))
            for i in range(3):
                stage_weight(i)
            stage_weight(3)

            def slot(s):
                e = s + 1
                if e.exists() and (e.has_before(1)):
                    load(e)
                e = s + -1
                if e.exists():
                    u = e.parity
                    if e.has_before(2):
                        after(mask_set, (e + -2).nth(1, 1))
                    else:
                        sp.wait_ge(consts_set, 5)
                    sp.dma_start(mask_u8[0:P:32, u, :],
                                 mask[e.number].partition_broadcast(4)).then_inc(mask_loaded[u], 16)
                e = s + -2
                if e.exists():
                    after(hid_set, e.nth(1, 1))
                    sp.dma_start(hidden[e.number], hid[:, e.parity, :]).then_inc(hid_stored[e.parity], 16)

            slots(sp, slot)
            for u in range(2):
                sp.wait_ge(hid_stored[u], 16 * (B // 2))

        @block.gpsimd
        def _(pool):
            pool.memset(ident[:], 0.0).then_inc(ident_zero, 1)
            pool.wait_ge(ident_zero, 1)
            pool.affine_select(out=ident[:], in_=ident[:], compare_op=ALU.not_equal, fill=1.0, base=0,
                               pattern=[[-1, P]], channel_multiplier=1).then_inc(ident_set, 1)
            pool.wait_ge(consts_set, 5)

            def slot(s):
                e = s + -1
                if e.exists():
                    pool.wait_ge(x1_set, e.nth(1, 1))
                    if e.has_before(2):
                        pool.wait_ge(hid_set, (e + -2).nth(1, 1))
                    else:
                        pool.wait_ge(biases_set, 3)
                    pool.tensor_tensor(x1b[:, e.parity, :], x1[:], attn_bias[:], ALU.add).then_inc(x1b_set, 1)
                e = s + 1
                if e.exists():
                    pool.wait_ge(in_veps, e.nth(1, 1))
                    if e.has_before(1):
                        pool.wait_ge(xn_ready, (e + -1).nth(2, 2))
                    pool.tensor_tensor(in_rstd[:], in_ve[:], neghalf[:], ALU.pow).then_inc(in_rstd_ready, 1)
                e = s
                if e.exists():
                    pool.wait_ge(x1_veps, e.nth(1, 1))
                    if e.has_before(1):
                        pool.wait_ge(x1n_set, (e + -1).nth(1, 1))
                    pool.tensor_tensor(x1_rstd[:], x1_ve[:], neghalf[:, 0:1], ALU.pow).then_inc(x1_rstd_ready, 1)

            slots(pool, slot)

        @block.scalar
        def _(act):
            act.wait_ge(small_in, 16 * SMALL_DMAS)
            for i in range(4):
                act.wait_ge(stage_in[i % 2], 16 * (i // 2 + 1))
                for c in range(DC):
                    scale = vecs[:, 0, c:c + 1] if i == Q_W else 1.0
                    act.activation(qkvc_hi[:, i, c, :], stage[:, i % 2, c, :], ACT.Identity,
                                   scale=scale).then_inc(w_hi_set, 1)

            def slot(s):
                e = s + -2
                if e.exists():
                    act.wait_ge(outT_turned, e.nth(1, 1))
                    act.activation(outT_hi[:].rearrange("p c n -> p (c n)"), bank[0][:], ACT.Copy)\
                       .then_inc(outT_hi_set, 1)
                e = s
                if e.exists():
                    act.wait_ge(ctxT_turned, e.nth(1, 1))
                    act.activation(ctxT_hi[:].rearrange("p c n -> p (c n)"), bank[1][:], ACT.Copy)\
                       .then_inc(ctxT_hi_set, 1)
                    act.wait_ge(m_done, e.nth(2, 1))
                    act.activation(mn_hi[:], bank[2][:], ACT.Identity, bias=bias0[:, 0:1]).then_inc(m_hi_set, 1)
                    act.wait_ge(m_done, e.nth(2, 2))
                    act.activation(mm_hi[:], bank[3][:], ACT.Identity, bias=bias0[:, 1:2]).then_inc(m_hi_set, 1)
                e = s + -1
                if e.exists():
                    act.wait_ge(xnT_turned, e.nth(1, 1))
                    act.activation(xnT_hi[:].rearrange("p c n -> p (c n)"), bank[5][:], ACT.Copy)\
                       .then_inc(xnT_hi_set, 1)

                def exp0(t):
                    e = s
                    if e.exists():
                        act.wait_ge(max0_set, e.nth(4, t + 1))
                        act.activation(A[:, t, :], bank[(6, 7, 1, 2)[t]][:], ACT.Exp, bias=negmax0[:, t:t + 1],
                                       accum_out=sum0[:, t:t + 1]).then_inc(exp0_done, 1)

                exp0(0)
                exp0(1)
                if e.exists():
                    act.wait_ge(q_done, e.nth(1, 1))
                    act.activation(q_sb[:], bank[0][:], ACT.Copy).then_inc(q_copied, 1)
                exp0(2)
                exp0(3)
                if e.exists():
                    for r in range(4):
                        act.wait_ge(shifted, e.nth(4, r + 1))
                        act.activation(probs[:, r, :, :], probs[:, r, :, :], ACT.Exp,
                                       scale=SCALE).then_inc(exp1_done, 1)
                e = s
                if e.exists():
                    act.wait_ge(k_done, e.nth(1, 1))
                    act.activation(k_sb[:], bank[0][:], ACT.Copy).then_inc(k_copied, 1)
                    act.wait_ge(v_done, e.nth(1, 1))
                    act.activation(v_sb[:, e.parity, :, 0:HD], bank[1][:].rearrange("p (h d) -> p h d", d=HD),
                                   ACT.Copy).then_inc(v_copied, 1)
                    for j in range(DC):
                        act.wait_ge(at_turned, e.nth(4, j + 1))
                        act.activation(at_hi[:, j, :], bank[2 + j][:], ACT.Copy).then_inc(at_hi_set, 1)
                    act.wait_ge(u_done, e.nth(1, 1))
                    act.activation(u_sb[:], bank[6][:], ACT.Copy).then_inc(u_copied, 1)
                e = s + -1
                if e.exists():
                    for r in range(4):
                        act.wait_ge(pT_turned, e.nth(4, r + 1))
                        act.activation(pT[:, r, :, :].rearrange("p c n -> p (c n)"), bank[r][:], ACT.Copy)\
                           .then_inc(pT_copied, 1)

            slots(act, slot)

        @block.vector
        def _(dve):
            dve.memset(ones[:], 1.0).then_inc(consts_set, 1)
            dve.memset(masked_bf[:], MASKED).then_inc(consts_set, 1)
            dve.memset(neghalf[:], -0.5).then_inc(consts_set, 1)
            dve.memset(mask_u8[:], 0).then_inc(consts_set, 1)
            dve.memset(v_sb[:, :, :, HD:HV], 1.0).then_inc(consts_set, 1)
            dve.wait_ge(consts_set, 5)
            dve.wait_ge(small_in, 16 * SMALL_DMAS)
            for c in range(DC):
                dve.tensor_scalar(vb_wide[:, c, :], ones[:], vecs[:, 4, c:c + 1], None,
                                  ALU.mult).then_inc(vb_wide_set, 1)
            for n, i in enumerate((0, 1, 3)):
                dve.wait_ge(small_turned, n + 1)
                dve.tensor_copy(small_t[:, i, :], bank[n][:, 0:P]).then_inc(small_copied, 1)
            dve.wait_ge(wow_done, 1)
            dve.tensor_copy(small_t[:, 2, :], bank[3][:, 0:P]).then_inc(wow_copied, 1)
            dve.wait_ge(wow_done, 2)
            dve.tensor_tensor(out0_bias[:], bank[4][:, 0:1], bias0[:, 3:4], ALU.add).then_inc(wow_copied, 1)

            def lower_halves(i):
                dve.wait_ge(stage_in[i % 2], 16 * (i // 2 + 1))
                for c in range(DC):
                    dve.wait_ge(w_hi_set, 4 * i + c + 1)
                    scale = vecs[:, 0, c:c + 1] if i == Q_W else 1.0
                    dve.scalar_tensor_tensor(out=qkvc_lo[:, i, c, :], in0=stage[:, i % 2, c, :], scalar=scale,
                                             in1=qkvc_hi[:, i, c, :].bitcast(F32), op0=ALU.mult,
                                             op1=ALU.subtract).then_inc(w_lo_set, 1)

            lower_halves(K_W)
            lower_halves(V_W)
            lower_halves(Q_W)
            dve.wait_ge(q_bias_done, 1)
            dve.tensor_tensor(q_bias[:], bank[5][:, 0:DC], vecs[:, 2, :], ALU.add).then_inc(biases_set, 2)
            lower_halves(C_W)
            dve.wait_ge(attn_bias_done, 1)
            dve.tensor_copy(attn_bias[:], bank[6][:]).then_inc(biases_set, 1)

            def lower(out, psum, hi, done):
                dve.tensor_tensor(out, psum, hi.bitcast(F32), ALU.subtract).then_inc(done, 1)

            def flat(t):
                return t[:].rearrange("p c n -> p (c n)")

            def slot(s):
                e = s + -2
                if e.exists():
                    dve.wait_ge(outT_hi_set, e.nth(1, 1))
                    lower(flat(outT_lo), bank[0][:], flat(outT_hi), outT_lo_set)
                e = s
                if e.exists():
                    dve.wait_ge(ctxT_hi_set, e.nth(1, 1))
                    lower(flat(ctxT_lo), bank[1][:], flat(ctxT_hi), ctxT_lo_set)
                    for i, (hi, lo) in enumerate(((mn_hi, mn_lo), (mm_hi, mm_lo))):
                        dve.wait_ge(m_hi_set, e.nth(2, i + 1))
                        dve.scalar_tensor_tensor(out=lo[:], in0=bank[2 + i][:], scalar=bias0[:, i:i + 1],
                                                 in1=hi[:].bitcast(F32), op0=ALU.add,
                                                 op1=ALU.subtract).then_inc(m_lo_set, 1)
                e = s + -1
                if e.exists():
                    dve.wait_ge(xnT_hi_set, e.nth(1, 1))
                    lower(flat(xnT_lo), bank[5][:], flat(xnT_hi), xnT_lo_set)
                    dve.wait_ge(mask_loaded[e.parity], e.dma())
                    if e.has_before(1):
                        dve.wait_ge(s1_done, (e + -1).nth(4, 4))
                    dve.tensor_scalar(mask_less_1[:], mask_u8[:, e.parity, :], -1.0, None,
                                      ALU.add).then_inc(mask_set, 1)

                def max0(t):
                    e = s
                    if e.exists():
                        dve.wait_ge(s0_done, e.nth(4, t + 1))
                        if t == 0 and e.has_before(1):
                            dve.wait_ge(exp0_done, (e + -1).nth(4, 4))
                        dve.tensor_reduce(negmax0[:, t:t + 1], bank[(6, 7, 1, 2)[t]][:], AX_X, ALU.max,
                                          negate=True).then_inc(max0_set, 1)

                max0(0)
                max0(1)
                e = s + -2
                if e.exists():
                    dve.wait_ge(cproj_done, e.nth(1, 1))
                    dve.wait_ge(x1b_set, e.nth(1, 1))
                    if e.has_before(2):
                        dve.wait_ge(hid_stored[e.parity], (e + -2).dma())
                    dve.tensor_tensor(hid[:, e.parity, :], bank[4][:], x1b[:, e.parity, :],
                                      ALU.add).then_inc(hid_set, 1)
                max0(2)
                max0(3)
                e = s + -1
                if e.exists():
                    dve.wait_ge(qT_turned, e.nth(1, 1))
                    dve.tensor_tensor(qT[:], bank[3][:].rearrange("p (c n) -> p c n", n=P),
                                      q_bias[:].unsqueeze(2).to_broadcast([P, DC, P]), ALU.add)\
                       .then_inc(qT_set, 1)
                if s.exists():
                    dve.wait_ge(exp0_done, s.nth(4, 4))
                    dve.reciprocal(rsum0[:], sum0[:]).then_inc(rsum0_set, 1)
                    dve.wait_ge(rsum0_set, s.nth(1, 1))
                    for t in range(DC):
                        dve.tensor_scalar(A[:, t, :], A[:, t, :], rsum0[:, t:t + 1], None,
                                          ALU.mult).then_inc(a_scaled, 1)
                if e.exists():
                    for r in range(4):
                        scores = bank[4 + r][:].rearrange("p (c n) -> p c n", n=P)
                        dve.wait_ge(s1_done, e.nth(4, r + 1))
                        dve.tensor_reduce(rowmax1[:, r, :], scores, AX_X, ALU.max).then_inc(max1_set, 1)
                        dve.wait_ge(max1_set, e.nth(4, r + 1))
                        if e.has_before(1):
                            dve.wait_ge(pT_turned, (e + -1).nth(4, r + 1))
                        dve.tensor_tensor(probs[:, r, :, :], scores,
                                          rowmax1[:, r, :].unsqueeze(2).to_broadcast([P, 4, P]),
                                          ALU.subtract).then_inc(shifted, 1)
                e = s + 1
                if e.exists():
                    u = e.parity
                    dve.wait_ge(x_loaded[u], e.dma())
                    dve.bn_stats(in_stats[:, 0, :], x_in[:, u, :]).then_inc(in_stat, 1)
                    dve.wait_ge(ctx_loaded[u], e.dma())
                    dve.bn_stats(in_stats[:, 1, :], ctx_in[:, u, :]).then_inc(in_stat, 1)
                    dve.wait_ge(in_stat, e.nth(2, 2))
                    dve.sem_inc(stats_seen, 1)
                    for i in range(2):
                        dve.bn_aggr(in_mv[:, i, :], in_stats[:, i, :]).then_inc(in_aggr, 1)
                    dve.wait_ge(in_aggr, e.nth(2, 2))
                    dve.tensor_scalar(in_ve[:], in_mv[:, :, 1], EPS, None, ALU.add).then_inc(in_veps, 1)
                    dve.wait_ge(in_rstd_ready, e.nth(1, 1))
                    if e.has_before(1):
                        dve.wait_ge(m_done, (e + -1).nth(2, 2))
                    for i, (src, dst) in enumerate(((x_in, xn), (ctx_in, cn))):
                        dve.tensor_scalar(dst[:], src[:, u, :], in_mv[:, i, 0:1], in_rstd[:, i:i + 1],
                                          ALU.subtract, ALU.mult).then_inc(xn_ready, 1)
                e = s
                if e.exists():
                    for j in range(DC):
                        dve.wait_ge(at_hi_set, e.nth(4, j + 1))
                        lower(at_lo[:, j, :], bank[2 + j][:], at_hi[:, j, :], at_lo_set)
                    dve.wait_ge(kT_turned, e.nth(1, 1))
                    dve.tensor_tensor(kT[:], bank[7][:].rearrange("p (c n) -> p c n", n=P),
                                      vecs[:, 3, :].unsqueeze(2).to_broadcast([P, DC, P]), ALU.add)\
                       .then_inc(kT_set, 1)
                e = s + -1
                if e.exists():
                    for g in range(2):
                        values = bank[4 + g][:, 0:8 * HV].rearrange("p (h d) -> p h d", d=HV)
                        dve.wait_ge(pv_done, e.nth(2, g + 1))
                        dve.reciprocal(rsum1[:, 8 * g:8 * g + 8], values[:, :, HD]).then_inc(rsum1_set, 1)
                        dve.wait_ge(rsum1_set, e.nth(2, g + 1))
                        dve.tensor_tensor(attn[:, 8 * g:8 * g + 8, :], values[:, :, 0:HD],
                                          rsum1[:, 8 * g:8 * g + 8].unsqueeze(2).to_broadcast([P, 8, HD]),
                                          ALU.mult).then_inc(attn_set, 1)
                e = s
                if e.exists():
                    dve.wait_ge(out0_done, e.nth(1, 1))
                    if e.has_before(1):
                        dve.wait_ge(x1b_set, (e + -1).nth(1, 1))
                    dve.scalar_tensor_tensor(out=x1[:], in0=bank[6][:], scalar=out0_bias[:, 0:1],
                                             in1=x_in[:, e.parity, :], op0=ALU.add, op1=ALU.add)\
                       .then_inc(x1_set, 1)
                    dve.wait_ge(x1_set, e.nth(1, 1))
                    dve.bn_stats(x1_stats[:], x1[:]).then_inc(x1_stat, 1)
                    dve.wait_ge(x1_stat, e.nth(1, 1))
                    dve.sem_inc(stats_seen, 1)
                    dve.bn_aggr(x1_mv[:], x1_stats[:]).then_inc(x1_aggr, 1)
                    dve.wait_ge(x1_aggr, e.nth(1, 1))
                    dve.tensor_scalar(x1_ve[:], x1_mv[:, 1:2], EPS, None, ALU.add).then_inc(x1_veps, 1)
                    dve.wait_ge(x1_rstd_ready, e.nth(1, 1))
                    dve.tensor_scalar(x1n[:], x1[:], x1_mv[:, 0:1], x1_rstd[:, 0:1],
                                      ALU.subtract, ALU.mult).then_inc(x1n_set, 1)

            slots(dve, slot)

        @block.tensor
        def _(pe):
            pe.wait_ge(small_in, 16 * SMALL_DMAS)
            pe.wait_ge(ident_set, 1)
            for n, i in enumerate((0, 1, 3)):
                pe.transpose(bank[n][:, 0:P], small[:, i, :], ident[:]).then_inc(small_turned, 1)
            pe.wait_ge(small_copied, 3)
            pe.matmul(bank[3][:, 0:P], small[:, 2, :], small_t[:, 3, :], start=True, stop=True).then_inc(wow_done, 1)
            pe.matmul(bank[4][:, 0:1], small_t[:, 3, :], bias0[:, 2:3], start=True, stop=True).then_inc(wow_done, 1)
            pe.wait_ge(stage_in[Q_W % 2], 32)
            for m in range(DC):
                for c in range(DC):
                    last = pe.matmul(bank[5][:, m:m + 1], stage[:, Q_W % 2, c, m * P:(m + 1) * P],
                                     vecs[:, 1, c:c + 1], start=(c == 0), stop=(c == DC - 1))
            last.then_inc(q_bias_done, 1)
            pe.wait_ge(stage_in[C_W % 2], 32)
            pe.wait_ge(vb_wide_set, DC)
            for c in range(DC):
                pe.matmul(bank[6][:], vb_wide[:, c, :], stage[:, C_W % 2, c, :], start=(c == 0), stop=False)
            pe.matmul(bank[6][:], ones[0:1, :], cb_row[:], start=False, stop=True).then_inc(attn_bias_done, 1)
            pe.wait_ge(w_lo_set, 16)
            pe.wait_ge(biases_set, 3)
            pe.wait_ge(wow_copied, 2)

            def turn(out, src, done):
                for c in range(DC):
                    last = pe.transpose(out[:, c * P:(c + 1) * P], src(c), ident[:])
                last.then_inc(done, 1)

            def project(out, hi, lo, weight, done):
                for c in range(DC):
                    last = three_passes(pe, out[:], hi[:, c, :], lo[:, c, :], qkvc_hi[:, weight, c, :],
                                        qkvc_lo[:, weight, c, :], c == 0, c == DC - 1)
                last.then_inc(done, 1)

            def slot(s):
                e0, e1, e2 = s, s + -1, s + -2

                if e2.exists():
                    pe.wait_ge(attn_set, e2.nth(2, 2))
                    turn(bank[0], lambda c: attn[:, 4 * c:4 * c + 4, :].rearrange("p h d -> p (h d)"), outT_turned)
                if e0.exists():
                    pe.wait_ge(ctx_loaded[e0.parity], e0.dma())
                    turn(bank[1], lambda c: ctx_in[:, e0.parity, c * P:(c + 1) * P], ctxT_turned)
                    pe.wait_ge(xn_ready, e0.nth(2, 1))
                    pe.matmul(bank[2][:], small_t[:, 0, :], xn[:], start=True, stop=True).then_inc(m_done, 1)
                    pe.wait_ge(xn_ready, e0.nth(2, 2))
                    pe.matmul(bank[3][:], small_t[:, 1, :], cn[:], start=True, stop=True).then_inc(m_done, 1)
                if e2.exists():
                    pe.wait_ge(outT_lo_set, e2.nth(1, 1))
                    project(bank[4], outT_hi, outT_lo, C_W, cproj_done)
                if e1.exists():
                    pe.wait_ge(x1n_set, e1.nth(1, 1))
                    turn(bank[5], lambda c: x1n[:, c * P:(c + 1) * P], xnT_turned)

                def s0(t):
                    if e0.exists():
                        if t == 0:
                            pe.wait_ge(m_lo_set, e0.nth(2, 2))
                            if e0.has_before(1):
                                pe.wait_ge(x1_set, (e0 + -1).nth(1, 1))
                        if t == 1 and e0.has_before(1):
                            pe.wait_ge(kT_set, (e0 + -1).nth(1, 1))
                        if t == 2:
                            pe.wait_ge(ctxT_lo_set, e0.nth(1, 1))
                        cols = slice(t * P, (t + 1) * P)
                        three_passes(pe, bank[(6, 7, 1, 2)[t]][:], mn_hi[:, cols], mn_lo[:, cols], mm_hi[:],
                                     mm_lo[:]).then_inc(s0_done, 1)

                s0(0)
                s0(1)
                if e1.exists():
                    pe.wait_ge(xnT_lo_set, e1.nth(1, 1))
                    project(bank[0], xnT_hi, xnT_lo, Q_W, q_done)
                s0(2)
                s0(3)
                if e1.exists():
                    pe.wait_ge(q_copied, e1.nth(1, 1))
                    turn(bank[3], lambda c: q_sb[:, c * P:(c + 1) * P], qT_turned)
                    pe.wait_ge(mask_set, e1.nth(1, 1))
                    if e2.exists():
                        pe.wait_ge(hid_set, e2.nth(1, 1))
                    pe.wait_ge(xnT_lo_set, e1.nth(1, 1))
                    if e0.exists():
                        pe.wait_ge(exp0_done, e0.nth(4, 2))
                    for r in range(4):
                        rows = slice(32 * r, 32 * r + 1)
                        pe.matmul(bank[4 + r][:].rearrange("p (c n) -> p c n", n=P), masked_bf[rows, :],
                                  mask_less_1[rows, :].unsqueeze(1).to_broadcast([1, 4, P]),
                                  start=True, stop=False)
                    pe.wait_ge(qT_set, e1.nth(1, 1))
                    pe.wait_ge(kT_set, e1.nth(1, 1))
                    for c in range(4):
                        for r in range(4):
                            rows = slice(32 * r, 32 * r + 32)
                            mm = pe.matmul(bank[4 + r][:, c * P:(c + 1) * P], qT[rows, c, :], kT[rows, c, :],
                                           start=False, stop=(c == 3))
                            if c == 3:
                                mm.then_inc(s1_done, 1)
                if e0.exists():
                    if e1.exists():
                        pe.wait_ge(q_copied, e1.nth(1, 1))
                    project(bank[0], ctxT_hi, ctxT_lo, K_W, k_done)
                    pe.wait_ge(exp0_done, e0.nth(4, 3))
                    project(bank[1], ctxT_hi, ctxT_lo, V_W, v_done)
                    pe.wait_ge(a_scaled, e0.nth(4, 4))
                    if e1.exists():
                        pe.wait_ge(qT_set, e1.nth(1, 1))
                        pe.wait_ge(shifted, e1.nth(4, 2))

                    def values0(j):
                        pe.wait_ge(at_lo_set, e0.nth(4, j + 1))
                        if j == 0 and e1.exists():
                            pe.wait_ge(shifted, e1.nth(4, 3))
                        return three_passes(pe, bank[6][:], ctxT_hi[:, j, :], ctxT_lo[:, j, :], at_hi[:, j, :],
                                            at_lo[:, j, :], j == 0, j == DC - 1)

                    for j in range(DC):
                        turn(bank[2 + j], lambda t: A[:, t, j * P:(j + 1) * P], at_turned)
                        if j >= 2:
                            values0(j - 2)
                    values0(DC - 2)
                    values0(DC - 1).then_inc(u_done, 1)
                    pe.wait_ge(k_copied, e0.nth(1, 1))
                    if e1.exists():
                        pe.wait_ge(shifted, e1.nth(4, 4))
                    turn(bank[7], lambda c: k_sb[:, c * P:(c + 1) * P], kT_turned)
                if e1.exists():
                    if e0.exists():
                        pe.wait_ge(v_copied, e0.nth(1, 1))
                    for r in range(4):
                        pe.wait_ge(exp1_done, e1.nth(4, r + 1))
                        turn(bank[r], lambda c: probs[:, r, c, :], pT_turned)
                if e0.exists():
                    pe.wait_ge(u_copied, e0.nth(1, 1))
                    pe.matmul(bank[6][:], small_t[:, 2, :], u_sb[:], start=True, stop=True).then_inc(out0_done, 1)
                if e1.exists():
                    pe.wait_ge(pT_copied, e1.nth(4, 4))
                    for h in range(HEADS):
                        g, i = h // 8, h % 8
                        mm = pe.matmul(bank[4 + g][:, i * HV:(i + 1) * HV], pT[:, h % 4, h // 4, :],
                                       v_sb[:, e1.parity, h, :], start=True, stop=True)
                        if i == 7:
                            mm.then_inc(pv_done, 1)

            slots(pe, slot)


def mlp_pass(nc, hidden, w, out):
    B, _, D = hidden.shape
    DC = D // P
    INNER = w["fc_w"].shape[1]
    IC = INNER // P
    TILES = 4
    N = TILES * P
    G = B // TILES

    with ExitStack() as stack:
        def sb(name, shape, dt=F32):
            return stack.enter_context(nc.sbuf_tensor(name, shape, dt))

        def sem(name):
            return stack.enter_context(nc.semaphore(name))

        acc = [stack.enter_context(nc.psum_tensor(f"acc{i}", [P, D], F32)) for i in range(TILES)]
        pre = [stack.enter_context(nc.psum_tensor(f"pre{i}", [P, N], F32)) for i in range(2)]
        tr = [stack.enter_context(nc.psum_tensor(f"tr{i}", [P, N], F32)) for i in range(2)]

        fc_hi = sb("fc_hi", [P, DC, INNER], F32R)
        fc_lo = sb("fc_lo", [P, DC, INNER], F32R)
        proj_hi = sb("proj_hi", [P, IC, D], F32R)
        proj_lo = sb("proj_lo", [P, IC, D], F32R)
        ln_vecs = sb("ln_vecs", [P, 2, DC])
        fc_bias = sb("fc_bias", [P, 2, IC])
        proj_bias = sb("proj_bias", [P, D])
        ident = sb("ident2", [P, P])
        neghalf = sb("neghalf2", [P, TILES])
        hid = sb("hid2", [P, 2, TILES, D])
        y = sb("y", [P, TILES, D])
        stats = sb("stats2", [P, TILES, 6])
        mv = sb("mv2", [P, TILES, 2])
        ve = sb("ve2", [P, TILES])
        rstd = sb("rstd2", [P, TILES])
        yT_hi = sb("yT_hi", [P, DC, N], F32R)
        yT_lo = sb("yT_lo", [P, DC, N], F32R)
        gl = sb("gl", [P, 2, N])
        hT_hi = sb("hT_hi", [P, 2, N], F32R)
        hT_lo = sb("hT_lo", [P, 2, N], F32R)

        vecs_in = sem("vecs_in")
        stage_in = [sem(f"wstage_in{i}") for i in range(2)]
        ident_zero = sem("ident_zero2")
        ident_set = sem("ident_set2")
        consts_set = sem("consts_set2")
        fc_b_done = sem("fc_b_done")
        fc_b_set = sem("fc_b_set")
        w_hi_set = sem("w_hi_set2")
        w_lo_set = sem("w_lo_set2")
        hid_loaded = [sem(f"hid_loaded{i}") for i in range(2)]
        out_stored = [sem(f"out_stored{i}") for i in range(2)]
        stat = sem("stat2")
        stats_seen = sem("stats_seen2")
        aggr = sem("aggr2")
        veps = sem("veps2")
        rstd_ready = sem("rstd_ready2")
        y_set = sem("y_set")
        bias_added = sem("bias_added")
        yT_turned = sem("yT_turned")
        yT_hi_set = sem("yT_hi_set")
        yT_lo_set = sem("yT_lo_set")
        fc_done = sem("fc_done")
        gelu_done = sem("gelu_done")
        hT_hi_set = sem("hT_hi_set")
        hT_lo_set = sem("hT_lo_set")
        proj_done = sem("proj_done")
        out_set = sem("out_set")

        stage = sb("wstage", [P, 2, 4, 512])
        fc_v = w["fc_w"].rearrange("(c p) n -> p c n", p=P)
        proj_v = w["proj_w"].rearrange("(c p) n -> p c n", p=P)
        STAGES = 8

        PAIRS = (G - 2) // 2

        def groups(eng, group):
            group(Item(0, 0, G))
            with eng.Fori(0, PAIRS) as pair:
                for g in range(1, 3):
                    group(Item(pair, g, G))
            for g in range(1 + 2 * PAIRS, G):
                group(Item(0, g, G))

        block = stack.enter_context(nc.Block())

        @block.sync
        def _(sp):
            for i, n in enumerate(("ln2_w", "ln2_b")):
                sp.dma_start(ln_vecs[:, i, :], w[n].rearrange("(c p) -> p c", p=P),
                             allow_slow_non_contiguous=True).then_inc(vecs_in, 16)
            sp.dma_start(fc_bias[:, 0, :], w["fc_b"].rearrange("(c p) -> p c", p=P),
                         allow_slow_non_contiguous=True).then_inc(vecs_in, 16)
            sp.dma_start(proj_bias[:], w["proj_b"].partition_broadcast(P)).then_inc(vecs_in, 16)

            def load(g):
                if g.has_before(2):
                    sp.wait_ge(out_stored[g.parity], (g + -2).dma(TILES))
                sp.dma_start(hid[:, g.parity, :, :],
                             hidden[bass.ds(g.number * TILES, TILES)].rearrange("t p n -> p t n"))\
                  .then_inc(hid_loaded[g.parity], 16)

            load(Item(0, 0, G))
            for i in range(STAGES):
                if i >= 2:
                    sp.wait_ge(w_lo_set, 4 * (i - 1))
                    sp.wait_ge(w_hi_set, 4 * (i - 1))
                    if i < 6:
                        sp.wait_ge(fc_b_done, i - 1)
                src = fc_v[:, i, :].rearrange("p (c n) -> p c n", n=512) if i < 4 else proj_v[:, 4 * (i - 4):4 * (i - 3), :]
                sp.dma_start(stage[:, i % 2, :, :], src).then_inc(stage_in[i % 2], 16)
            load(Item(0, 1, G))

            def group(g):
                if (g + 1).exists() and g.has_before(1):
                    load(g + 1)
                for t in range(TILES):
                    sp.wait_ge(out_set, g.nth(TILES, t + 1))
                    sp.dma_start(out[g.number * TILES + t], hid[:, g.parity, t, :])\
                      .then_inc(out_stored[g.parity], 16)

            groups(sp, group)
            for u in range(2):
                sp.wait_ge(out_stored[u], 16 * TILES * (G // 2))

        @block.gpsimd
        def _(pool):
            pool.memset(ident[:], 0.0).then_inc(ident_zero, 1)
            pool.wait_ge(ident_zero, 1)
            pool.affine_select(out=ident[:], in_=ident[:], compare_op=ALU.not_equal, fill=1.0, base=0,
                               pattern=[[-1, P]], channel_multiplier=1).then_inc(ident_set, 1)
            pool.wait_ge(consts_set, 1)
            pool.wait_ge(vecs_in, 16 * 4)

            def prepare(g):
                pool.wait_ge(veps, g.nth(1, 1))
                if g.has_before(1):
                    pool.wait_ge(y_set, (g + -1).nth(4, 4))
                pool.tensor_tensor(rstd[:], ve[:], neghalf[:], ALU.pow).then_inc(rstd_ready, 1)
                for t in range(TILES):
                    pool.wait_ge(y_set, g.nth(4, t + 1))
                    pool.tensor_tensor(hid[:, g.parity, t, :], hid[:, g.parity, t, :], proj_bias[:],
                                       ALU.add).then_inc(bias_added, 1)

            prepare(Item(0, 0, G))

            def group(g):
                if (g + 1).exists():
                    prepare(g + 1)

            groups(pool, group)

        @block.scalar
        def _(act):
            act.wait_ge(vecs_in, 16 * 4)
            for i in range(STAGES):
                act.wait_ge(stage_in[i % 2], 16 * (i // 2 + 1))
                for c in range(4):
                    dst = fc_hi[:, i, c * 512:(c + 1) * 512] if i < 4 else proj_hi[:, 4 * (i - 4) + c, :]
                    act.activation(dst, stage[:, i % 2, c, :], ACT.Identity,
                                   scale=ln_vecs[:, 0, i:i + 1] if i < 4 else 1.0).then_inc(w_hi_set, 1)

            def turned(g):
                for c in range(DC):
                    act.wait_ge(yT_turned, g.nth(4, c + 1))
                    act.activation(yT_hi[:, c, :], tr[c % 2][:], ACT.Copy).then_inc(yT_hi_set, 1)

            turned(Item(0, 0, G))
            act.wait_ge(fc_b_set, 2)

            def group(g):
                for i in range(IC):
                    act.wait_ge(fc_done, g.nth(IC, i + 1))
                    if i >= 2:
                        act.wait_ge(hT_lo_set, g.nth(IC, i - 1))
                    elif g.has_before(1):
                        act.wait_ge(hT_lo_set, (g + -1).nth(IC, IC - 1 + i))
                    act.activation(gl[:, i % 2, :], pre[i % 2][:], ACT.Gelu_apprx_tanh,
                                   bias=fc_bias[:, 1, i:i + 1]).then_inc(gelu_done, 1)
                if (g + 1).exists():
                    turned(g + 1)

            groups(act, group)

        @block.vector
        def _(dve):
            dve.memset(neghalf[:], -0.5).then_inc(consts_set, 1)
            dve.wait_ge(vecs_in, 16 * 4)

            def statistics(g, t):
                if t == 0:
                    dve.wait_ge(hid_loaded[g.parity], g.dma())
                dve.bn_stats(stats[:, t, :], hid[:, g.parity, t, :]).then_inc(stat, 1)
                if t == TILES - 1:
                    dve.wait_ge(stat, g.nth(4, 4))
                    dve.sem_inc(stats_seen, 1)
                    for i in range(TILES):
                        dve.bn_aggr(mv[:, i, :], stats[:, i, :]).then_inc(aggr, 1)
                    dve.wait_ge(aggr, g.nth(4, 4))
                    dve.tensor_scalar(ve[:], mv[:, :, 1], EPS, None, ALU.add).then_inc(veps, 1)

            def normalise(g, t):
                if t == 0:
                    dve.wait_ge(rstd_ready, g.nth(1, 1))
                    if g.has_before(1):
                        dve.wait_ge(yT_turned, (g + -1).nth(4, 4))
                dve.tensor_scalar(y[:, t, :], hid[:, g.parity, t, :], mv[:, t, 0:1], rstd[:, t:t + 1],
                                  ALU.subtract, ALU.mult).then_inc(y_set, 1)

            def turned(g):
                for c in range(DC):
                    dve.wait_ge(yT_hi_set, g.nth(4, c + 1))
                    dve.tensor_tensor(yT_lo[:, c, :], tr[c % 2][:], yT_hi[:, c, :].bitcast(F32),
                                      ALU.subtract).then_inc(yT_lo_set, 1)

            first = Item(0, 0, G)
            for t in range(TILES):
                statistics(first, t)
            for t in range(TILES):
                normalise(first, t)
            for i in range(STAGES):
                dve.wait_ge(stage_in[i % 2], 16 * (i // 2 + 1))
                for c in range(4):
                    dve.wait_ge(w_hi_set, 4 * i + c + 1)
                    cols = slice(c * 512, (c + 1) * 512)
                    lo = fc_lo[:, i, cols] if i < 4 else proj_lo[:, 4 * (i - 4) + c, :]
                    hi = fc_hi[:, i, cols] if i < 4 else proj_hi[:, 4 * (i - 4) + c, :]
                    dve.scalar_tensor_tensor(out=lo, in0=stage[:, i % 2, c, :],
                                             scalar=ln_vecs[:, 0, i:i + 1] if i < 4 else 1.0,
                                             in1=hi.bitcast(F32), op0=ALU.mult,
                                             op1=ALU.subtract).then_inc(w_lo_set, 1)
            dve.wait_ge(fc_b_done, DC)
            dve.tensor_reduce(fc_bias[:, 1, :], acc[0][:, 0:DC * IC].rearrange("p (c i) -> p i c", c=DC),
                              AX_X, ALU.add).then_inc(fc_b_set, 1)
            dve.wait_ge(fc_b_set, 1)
            dve.tensor_tensor(fc_bias[:, 1, :], fc_bias[:, 1, :], fc_bias[:, 0, :], ALU.add).then_inc(fc_b_set, 1)
            turned(first)

            def group(g):
                nxt = g + 1
                for i in range(IC):
                    dve.wait_ge(gelu_done, g.nth(IC, i + 1))
                    if i >= 2:
                        dve.wait_ge(proj_done, g.nth(IC, i - 1))
                    elif g.has_before(1):
                        dve.wait_ge(proj_done, (g + -1).nth(IC, IC - 1 + i))
                    dve.tensor_copy(hT_hi[:, i % 2, :], gl[:, i % 2, :]).then_inc(hT_hi_set, 1)
                    dve.wait_ge(hT_hi_set, g.nth(IC, i + 1))
                    dve.tensor_tensor(hT_lo[:, i % 2, :], gl[:, i % 2, :], hT_hi[:, i % 2, :].bitcast(F32),
                                      ALU.subtract).then_inc(hT_lo_set, 1)
                    if nxt.exists():
                        if 3 <= i < 3 + TILES:
                            statistics(nxt, i - 3)
                        if 9 <= i < 9 + TILES:
                            normalise(nxt, i - 9)
                if nxt.exists():
                    turned(nxt)
                for t in range(TILES):
                    if t == 0:
                        dve.wait_ge(proj_done, g.nth(IC, IC))
                    dve.wait_ge(bias_added, g.nth(4, t + 1))
                    dve.tensor_tensor(hid[:, g.parity, t, :], acc[t][:], hid[:, g.parity, t, :],
                                      ALU.add).then_inc(out_set, 1)

            groups(dve, group)

        @block.tensor
        def _(pe):
            pe.wait_ge(ident_set, 1)
            pe.wait_ge(vecs_in, 16 * 4)

            def turn(g, c):
                if c == 0:
                    pe.wait_ge(y_set, g.nth(4, 4))
                if c >= 2:
                    pe.wait_ge(yT_lo_set, g.nth(4, c - 1))
                elif g.has_before(1):
                    pe.wait_ge(yT_lo_set, (g + -1).nth(4, c + 3))
                for t in range(TILES):
                    last = pe.transpose(tr[c % 2][:, t * P:(t + 1) * P], y[:, t, c * P:(c + 1) * P], ident[:])
                last.then_inc(yT_turned, 1)

            for c in range(DC):
                pe.wait_ge(stage_in[c % 2], 16 * (c // 2 + 1))
                for i in range(IC):
                    last = pe.matmul(acc[0][:, c * IC + i:c * IC + i + 1],
                                     stage[:, c % 2, i // 4, (i % 4) * P:(i % 4 + 1) * P],
                                     ln_vecs[:, 1, c:c + 1], start=True, stop=True)
                last.then_inc(fc_b_done, 1)
            for c in range(DC):
                turn(Item(0, 0, G), c)
            pe.wait_ge(w_lo_set, 4 * STAGES)
            pe.wait_ge(fc_b_set, 1)

            def three_passes(out, a_hi, a_lo, b_hi, b_lo, first, last):
                pe.matmul(out, a_hi, b_lo, start=first, stop=False)
                pe.matmul(out, a_lo, b_hi, start=False, stop=False)
                return pe.matmul(out, a_hi, b_hi, start=False, stop=last)

            def fc(g, i):
                if i == 0:
                    pe.wait_ge(yT_lo_set, g.nth(4, 4))
                if i >= 2:
                    pe.wait_ge(gelu_done, g.nth(IC, i - 1))
                elif g.has_before(1):
                    pe.wait_ge(gelu_done, (g + -1).nth(IC, IC - 1 + i))
                cols = slice(i * P, (i + 1) * P)
                for c in range(DC):
                    last = three_passes(pre[i % 2][:], fc_hi[:, c, cols], fc_lo[:, c, cols], yT_hi[:, c, :],
                                        yT_lo[:, c, :], c == 0, c == DC - 1)
                last.then_inc(fc_done, 1)

            def proj(g, i):
                pe.wait_ge(hT_lo_set, g.nth(IC, i + 1))
                if i == 0 and g.has_before(1):
                    pe.wait_ge(out_set, (g + -1).nth(4, 4))
                for t in range(TILES):
                    cols = slice(t * P, (t + 1) * P)
                    last = three_passes(acc[t][:], hT_hi[:, i % 2, cols], hT_lo[:, i % 2, cols], proj_hi[:, i, :],
                                        proj_lo[:, i, :], i == 0, i == IC - 1)
                last.then_inc(proj_done, 1)

            def group(g):
                more = (g + 1).exists()
                for i in range(IC):
                    fc(g, i)
                    if i == IC - 1 and more:
                        turn(g + 1, 0)
                        turn(g + 1, 1)
                    if i >= 1:
                        proj(g, i - 1)
                if more:
                    turn(g + 1, 2)
                    turn(g + 1, 3)
                proj(g, IC - 1)

            groups(pe, group)


def kernel(**inputs):
    import numpy as np
    import concourse.bacc as bacc
    from concourse.bass_utils import run_bass_kernel_spmd

    nc = bacc.Bacc("TRN2", target_bir_lowering=False, num_devices=1)
    arrays, aps = {}, {}
    for name, value in inputs.items():
        a = np.ascontiguousarray(value)
        if a.dtype == np.bool_:
            a = a.view(np.uint8)
        arrays[f"in_{name}"] = a
        aps[name] = nc.dram_tensor(f"in_{name}", a.shape, mybir.dt.from_np(a.dtype), kind="ExternalInput").ap()
    shape = inputs["x"].shape
    out = nc.dram_tensor("out", shape, F32, kind="ExternalOutput").ap()
    hidden = nc.dram_tensor("hidden", shape, F32, kind="Internal").ap()
    w = {name.split("_xattn_", 1)[1]: ap for name, ap in aps.items() if "_xattn_" in name}
    attention_pass(nc, aps["x"], aps["ctx_2048"], aps["mask_BxS2_bf1"], w, hidden)
    mlp_pass(nc, hidden, w, out)
    r = run_bass_kernel_spmd(nc, [arrays], core_ids=[0])
    return r.results[0]["out"]
```

```python
from contextlib import ExitStack

import concourse.bass as bass
from concourse import mybir

F32 = mybir.dt.float32
F32R = mybir.dt.float32r
BF16 = mybir.dt.bfloat16
U8 = mybir.dt.uint8
ALU = mybir.AluOpType
ACT = mybir.ActivationFunctionType
AX_X = mybir.AxisListType.X

P = 128
EPS = 1e-5
HEADS = 16
STAGE = 4
MASKED = 3.3895313892515355e38


class Item:

    def __init__(self, pair, offset, count):
        self.pair, self.offset, self.count = pair, offset, count

    def __add__(self, k):
        return Item(self.pair, self.offset + k, self.count)

    def exists(self):
        return not isinstance(self.pair, int) or 0 <= self.offset < self.count

    def has_before(self, k=1):
        return not isinstance(self.pair, int) or self.offset - k >= 0

    @property
    def parity(self):
        return self.offset % 2

    @property
    def number(self):
        return self.pair * 2 + self.offset

    def nth(self, per_item, k):
        return self.pair * (2 * per_item) + (self.offset * per_item + k)

    def dma(self, k=1):
        return self.pair * (16 * k) + (self.offset // 2 + 1) * (16 * k)


def mlp_stage_source(w, n):
    if n % 2 == 0:
        return w["fc_w"].rearrange("(c p) n -> p c n", p=P)[:, :, (n // 2) * 512:(n // 2 + 1) * 512]
    return w["proj_w"].rearrange("(c p) n -> p c n", p=P)[:, STAGE * (n // 2):STAGE * (n // 2 + 1), :]


def attention_pass(nc, x, ctx, mask, w, hidden, stage, mlp_staged):
    B, C, T = x.shape
    D = T
    DC = D // P
    HD = D // HEADS
    SCALE = float(HD) ** -0.5
    assert C == P and D == 4 * P and HD == 32

    with ExitStack() as stack:
        def sb(name, shape, dt=F32):
            return stack.enter_context(nc.sbuf_tensor(name, shape, dt))

        def sem(name):
            return stack.enter_context(nc.semaphore(name))

        bank = [stack.enter_context(nc.psum_tensor(f"bank{i}", [P, 512], F32)) for i in range(8)]

        qkvc_hi = sb("qkvc_hi", [P, 4, DC, D], F32R)
        qkvc_lo = sb("qkvc_lo", [P, 4, DC, D], F32R)
        small = sb("small", [P, 4, P])
        small_t = sb("small_t", [P, 4, P])
        small_hi = sb("small_hi", [P, 3, P], F32R)
        small_lo = sb("small_lo", [P, 3, P], F32R)
        vecs = sb("vecs", [P, 5, DC])
        q_scale = sb("q_scale", [P, DC])
        bias0 = sb("bias0", [P, 4])
        out0_bias = sb("out0_bias", [P, 1])
        q_bias = sb("q_bias", [P, DC])
        vb_wide = sb("vb_wide", [P, DC, P])
        cb_row = sb("cb_row", [1, D])
        attn_bias = sb("attn_bias", [P, D])
        ident = sb("ident", [P, P])
        ones = sb("ones", [P, P])
        masked_bf = sb("masked_bf", [P, P], BF16)
        neghalf = sb("neghalf", [P, 2])

        x_in = sb("x_in", [P, 2, T])
        ctx_in = sb("ctx_in", [P, 2, T])
        in_stats = sb("in_stats", [P, 2, 6])
        in_mv = sb("in_mv", [P, 2, 2])
        in_ve = sb("in_ve", [P, 2])
        in_rstd = sb("in_rstd", [P, 2])
        normed = sb("normed", [P, 2, T])
        normed_hi = sb("normed_hi", [P, 2, T], F32R)
        normed_lo = sb("normed_lo", [P, 2, T], F32R)
        m_hi = sb("m_hi", [P, 2, T], F32R)
        m_lo = sb("m_lo", [P, 2, T], F32R)
        ctxT_hi = sb("ctxT_hi", [P, DC, P], F32R)
        ctxT_lo = sb("ctxT_lo", [P, DC, P], F32R)
        negmax0 = sb("negmax0", [P, DC])
        sum0 = sb("sum0", [P, DC])
        rsum0 = sb("rsum0", [P, DC])
        A = sb("A", [P, DC, T])
        at_hi = sb("at_hi", [P, DC, T], F32R)
        at_lo = sb("at_lo", [P, DC, T], F32R)
        u_hi = sb("u_hi", [P, T], F32R)
        u_lo = sb("u_lo", [P, T], F32R)
        x1 = sb("x1", [P, D])
        x1_stats = sb("x1_stats", [P, 6])
        x1_mv = sb("x1_mv", [P, 2])
        x1_ve = sb("x1_ve", [P, 1])
        x1_rstd = sb("x1_rstd", [P, 1])
        x1b = sb("x1b", [P, 2, D])
        x1n = sb("x1n", [P, D])
        xnT_hi = sb("xnT_hi", [P, DC, P], F32R)
        xnT_lo = sb("xnT_lo", [P, DC, P], F32R)
        q_sb = sb("q_sb", [P, D])
        k_sb = sb("k_sb", [P, D])
        qT = sb("qT", [P, DC, P])
        kT = sb("kT", [P, DC, P])
        v_sb = sb("v_sb", [P, 2, D])
        mask_u8 = sb("mask_u8", [P, 2, P], U8)
        mask_less_1 = sb("mask_less_1", [P, P], BF16)
        negmax1 = sb("negmax1", [P, 4, 4])
        sum1 = sb("sum1", [P, 4, 4])
        rsum1 = sb("rsum1", [P, 4, 4])
        probs = sb("probs", [P, 4, 4, P])
        pT = sb("pT", [P, 4, 4, P])
        outT_hi = sb("outT_hi", [P, DC, P], F32R)
        outT_lo = sb("outT_lo", [P, DC, P], F32R)
        hid = sb("hid", [P, 2, D])

        sp_steps = sem("sp_steps")
        small_in = sem("small_in")
        stage_in = [sem(f"stage_in{i}") for i in range(2)]
        consts_set = sem("consts_set")
        ident_zero = sem("ident_zero")
        ident_set = sem("ident_set")
        vb_wide_set = sem("vb_wide_set")
        small_turned = sem("small_turned")
        small_copied = sem("small_copied")
        wow_done = sem("wow_done")
        wow_copied = sem("wow_copied")
        small_hi_set = sem("small_hi_set")
        small_lo_set = sem("small_lo_set")
        q_scale_set = sem("q_scale_set")
        q_bias_done = sem("q_bias_done")
        q_bias_set = sem("q_bias_set")
        attn_bias_done = sem("attn_bias_done")
        attn_bias_set = sem("attn_bias_set")
        w_hi_set = sem("w_hi_set")
        w_lo_set = sem("w_lo_set")
        x_loaded = [sem(f"x_loaded{i}") for i in range(2)]
        ctx_loaded = [sem(f"ctx_loaded{i}") for i in range(2)]
        mask_loaded = [sem(f"mask_loaded{i}") for i in range(2)]
        hid_stored = [sem(f"hid_stored{i}") for i in range(2)]
        in_stat = sem("in_stat")
        stats_seen = sem("stats_seen")
        in_aggr = sem("in_aggr")
        in_veps = sem("in_veps")
        in_rstd_ready = sem("in_rstd_ready")
        normed_set = sem("normed_set")
        normed_hi_set = sem("normed_hi_set")
        normed_lo_set = sem("normed_lo_set")
        ctxT_turned = sem("ctxT_turned")
        ctxT_hi_set = sem("ctxT_hi_set")
        ctxT_lo_set = sem("ctxT_lo_set")
        m_done = sem("m_done")
        m_hi_set = sem("m_hi_set")
        m_lo_set = sem("m_lo_set")
        s0_done = sem("s0_done")
        max0_set = sem("max0_set")
        exp0_done = sem("exp0_done")
        rsum0_set = sem("rsum0_set")
        a_scaled = sem("a_scaled")
        at_turned = sem("at_turned")
        at_hi_set = sem("at_hi_set")
        at_lo_set = sem("at_lo_set")
        u_done = sem("u_done")
        u_hi_set = sem("u_hi_set")
        u_lo_set = sem("u_lo_set")
        out0_done = sem("out0_done")
        x1_set = sem("x1_set")
        x1_stat = sem("x1_stat")
        x1_aggr = sem("x1_aggr")
        x1_veps = sem("x1_veps")
        x1_rstd_ready = sem("x1_rstd_ready")
        x1n_set = sem("x1n_set")
        x1b_set = sem("x1b_set")
        xnT_turned = sem("xnT_turned")
        xnT_hi_set = sem("xnT_hi_set")
        xnT_lo_set = sem("xnT_lo_set")
        q_done = sem("q_done")
        q_copied = sem("q_copied")
        qT_turned = sem("qT_turned")
        qT_set = sem("qT_set")
        k_done = sem("k_done")
        k_copied = sem("k_copied")
        kT_turned = sem("kT_turned")
        kT_set = sem("kT_set")
        v_done = sem("v_done")
        v_copied = sem("v_copied")
        mask_set = sem("mask_set")
        s1_done = sem("s1_done")
        max1_set = sem("max1_set")
        exp1_done = sem("exp1_done")
        rsum1_set = sem("rsum1_set")
        probs_set = sem("probs_set")
        pT_turned = sem("pT_turned")
        pT_copied = sem("pT_copied")
        outT_done = sem("outT_done")
        outT_hi_set = sem("outT_hi_set")
        outT_lo_set = sem("outT_lo_set")
        cproj_done = sem("cproj_done")
        hid_set = sem("hid_set")

        SMALL_DMAS = 4 + 5 + 4 + 1
        WEIGHTS = ("k_w", "v_w", "q_w", "cproj_w")
        K_W, V_W, Q_W, C_W = range(4)
        S0_BANK = (5, 6, 0, 1)
        S1_BANK = (2, 4, 5, 6)
        AT_BANK = (1, 3, 2, 4)
        PT_BANK = (1, 3, 5, 6)

        FIRST, LOOPED, LAST = -1, 3, B + 1
        PAIRS = (B - 1 - LOOPED) // 2

        def slots(eng, slot, ahead=None):
            for s in range(FIRST, LOOPED):
                if ahead and s in ahead:
                    ahead[s]()
                slot(Item(0, s, B))
            with eng.Fori(0, PAIRS) as pair:
                for s in range(LOOPED, LOOPED + 2):
                    slot(Item(pair, s, B))
            for s in range(LOOPED + 2 * PAIRS, LAST + 1):
                slot(Item(0, s, B))

        def flat(t):
            return t[:].rearrange("p c n -> p (c n)")

        def by_chunk(b):
            return bank[b][:].rearrange("p (c n) -> p c n", n=P)

        block = stack.enter_context(nc.Block())

        @block.sync
        def _(sp):
            def after(semaphore, value):
                sp.wait_ge(semaphore, value)
                sp.sem_inc(sp_steps, 1)

            def load(e):
                if e.has_before(2):
                    after(x1_set, (e + -2).nth(1, 1))
                    after(ctxT_turned, (e + -2).nth(1, 1))
                    after(normed_set, (e + -2).nth(2, 2))
                u = e.parity
                sp.dma_start(x_in[:, u, :], x[e.number]).then_inc(x_loaded[u], 16)
                sp.dma_start(ctx_in[:, u, :], ctx[e.number]).then_inc(ctx_loaded[u], 16)

            def stage_weight(i):
                if i >= 2:
                    sp.wait_ge(w_hi_set, 4 * (i - 1))
                    sp.wait_ge(w_lo_set, 4 * (i - 1))
                sp.dma_start(stage[:, i % 2, :, :],
                             w[WEIGHTS[i]].rearrange("(c p) n -> p c n", p=P)).then_inc(stage_in[i % 2], 16)

            load(Item(0, 0, B))
            for i, n in enumerate(("Wn", "Wm", "Wl", "Wo")):
                sp.dma_start(small[:, i, :], w[n]).then_inc(small_in, 16)
            for i, n in enumerate(("ln1_w", "ln1_b", "q_b", "k_b", "v_b")):
                sp.dma_start(vecs[:, i, :], w[n].rearrange("(c p) -> p c", p=P),
                             allow_slow_non_contiguous=True).then_inc(small_in, 16)
            for i, n in enumerate(("bn", "bm", "bl", "bo")):
                sp.dma_start(bias0[:, i:i + 1], w[n].rearrange("(p a) -> p a", a=1)).then_inc(small_in, 16)
            sp.dma_start(cb_row[:], w["cproj_b"].rearrange("(a d) -> a d", a=1)).then_inc(small_in, 16)
            stage_weight(0)
            stage_weight(1)
            load(Item(0, 1, B))
            stage_weight(2)
            stage_weight(3)

            def slot(s):
                e = s + 1
                if e.exists() and e.has_before(2):
                    load(e)
                e = s + -1
                if e.exists():
                    u = e.parity
                    if e.has_before(2):
                        after(mask_set, (e + -2).nth(1, 1))
                    else:
                        sp.wait_ge(consts_set, 4)
                    sp.dma_start(mask_u8[0:P:32, u, :],
                                 mask[e.number].partition_broadcast(4)).then_inc(mask_loaded[u], 16)
                e = s + -2
                if e.exists():
                    after(hid_set, e.nth(1, 1))
                    sp.dma_start(hidden[e.number], hid[:, e.parity, :]).then_inc(hid_stored[e.parity], 16)

            slots(sp, slot)
            sp.wait_ge(w_hi_set, 16)
            sp.wait_ge(w_lo_set, 16)
            sp.wait_ge(attn_bias_done, 1)
            for n in range(2):
                sp.dma_start(stage[:, n, :, :], mlp_stage_source(w, n)).then_inc(mlp_staged[n], 16)
            for u in range(2):
                sp.wait_ge(hid_stored[u], 16 * (B // 2))
                sp.wait_ge(mlp_staged[u], 16)

        @block.gpsimd
        def _(pool):
            pool.memset(ident[:], 0.0).then_inc(ident_zero, 1)
            pool.wait_ge(ident_zero, 1)
            pool.affine_select(out=ident[:], in_=ident[:], compare_op=ALU.not_equal, fill=1.0, base=0,
                               pattern=[[-1, P]], channel_multiplier=1).then_inc(ident_set, 1)
            pool.wait_ge(consts_set, 4)

            def slot(s):
                e = s + -1
                if e.exists():
                    pool.wait_ge(x1_set, e.nth(1, 1))
                    if e.has_before(2):
                        pool.wait_ge(hid_set, (e + -2).nth(1, 1))
                    else:
                        pool.wait_ge(attn_bias_set, 1)
                    pool.tensor_tensor(x1b[:, e.parity, :], x1[:], attn_bias[:], ALU.add).then_inc(x1b_set, 1)
                e = s + 1
                if e.exists():
                    pool.wait_ge(in_veps, e.nth(1, 1))
                    if e.has_before(1):
                        pool.wait_ge(normed_set, (e + -1).nth(2, 2))
                    pool.tensor_tensor(in_rstd[:], in_ve[:], neghalf[:], ALU.pow).then_inc(in_rstd_ready, 1)
                    for i in range(2):
                        pool.wait_ge(normed_hi_set, e.nth(2, i + 1))
                        if e.has_before(1):
                            pool.wait_ge(m_done, (e + -1).nth(2, 2))
                        pool.tensor_tensor(normed_lo[:, i, :], normed[:, i, :], normed_hi[:, i, :].bitcast(F32),
                                           ALU.subtract).then_inc(normed_lo_set, 1)
                e = s + -1
                if e.exists():
                    for r in range(4):
                        pool.wait_ge(rsum1_set, e.nth(4, r + 1))
                        pool.tensor_tensor(probs[:, r, :, :], probs[:, r, :, :],
                                           rsum1[:, r, :].unsqueeze(2).to_broadcast([P, 4, P]),
                                           ALU.mult).then_inc(probs_set, 1)
                e = s
                if e.exists():
                    pool.wait_ge(x1_veps, e.nth(1, 1))
                    if e.has_before(1):
                        pool.wait_ge(x1n_set, (e + -1).nth(1, 1))
                    pool.tensor_tensor(x1_rstd[:], x1_ve[:], neghalf[:, 0:1], ALU.pow).then_inc(x1_rstd_ready, 1)

            slots(pool, slot)

        @block.scalar
        def _(act):
            act.wait_ge(small_in, 16 * SMALL_DMAS)

            def upper_halves(i):
                act.wait_ge(stage_in[i % 2], 16 * (i // 2 + 1))
                if i == Q_W:
                    act.wait_ge(q_scale_set, 1)
                for c in range(DC):
                    act.activation(qkvc_hi[:, i, c, :], stage[:, i % 2, c, :], ACT.Identity,
                                   scale=q_scale[:, c:c + 1] if i == Q_W else 1.0).then_inc(w_hi_set, 1)

            def slot(s):
                e0, e1 = s, s + -1
                if e0.exists():
                    act.wait_ge(ctxT_turned, e0.nth(1, 1))
                    act.activation(flat(ctxT_hi), bank[0][:], ACT.Copy).then_inc(ctxT_hi_set, 1)
                    for i, b in enumerate((1, 3)):
                        act.wait_ge(m_done, e0.nth(2, i + 1))
                        act.activation(m_hi[:, i, :], bank[b][:], ACT.Identity,
                                       bias=bias0[:, i:i + 1]).then_inc(m_hi_set, 1)
                if e1.exists():
                    act.wait_ge(xnT_turned, e1.nth(1, 1))
                    act.activation(flat(xnT_hi), bank[4][:], ACT.Copy).then_inc(xnT_hi_set, 1)

                def exp0(t):
                    if e0.exists():
                        act.wait_ge(max0_set, e0.nth(4, t + 1))
                        act.activation(A[:, t, :], bank[S0_BANK[t]][:], ACT.Exp, bias=negmax0[:, t:t + 1],
                                       accum_out=sum0[:, t:t + 1]).then_inc(exp0_done, 1)

                exp0(0)
                exp0(1)
                if e1.exists():
                    act.wait_ge(q_done, e1.nth(1, 1))
                    act.activation(q_sb[:], bank[7][:], ACT.Copy).then_inc(q_copied, 1)
                exp0(2)
                exp0(3)

                def exp1(r):
                    if e1.exists():
                        act.wait_ge(max1_set, e1.nth(4, r + 1))
                        if e1.has_before(1):
                            act.wait_ge(pT_turned, (e1 + -1).nth(4, r + 1))
                        for c in range(4):
                            act.activation(probs[:, r, c, :], by_chunk(S1_BANK[r])[:, c, :], ACT.Exp,
                                           bias=negmax1[:, r, c:c + 1],
                                           accum_out=sum1[:, r, c:c + 1]).then_inc(exp1_done, 1)

                def at_upper(j):
                    if e0.exists():
                        act.wait_ge(at_turned, e0.nth(4, j + 1))
                        act.activation(at_hi[:, j, :], bank[AT_BANK[j]][:], ACT.Copy).then_inc(at_hi_set, 1)

                def copy_pT(r):
                    if e1.exists():
                        act.wait_ge(pT_turned, e1.nth(4, r + 1))
                        act.activation(pT[:, r, :, :].rearrange("p c n -> p (c n)"), bank[PT_BANK[r]][:],
                                       ACT.Copy).then_inc(pT_copied, 1)

                exp1(0)
                exp1(1)
                at_upper(0)
                exp1(2)
                if e0.exists():
                    act.wait_ge(v_done, e0.nth(1, 1))
                    act.activation(v_sb[:, e0.parity, :], bank[0][:], ACT.Copy).then_inc(v_copied, 1)
                at_upper(1)
                at_upper(2)
                at_upper(3)
                exp1(3)
                copy_pT(0)
                copy_pT(1)
                if e0.exists():
                    act.wait_ge(u_done, e0.nth(1, 1))
                    act.activation(u_hi[:], bank[7][:], ACT.Copy).then_inc(u_hi_set, 1)
                copy_pT(2)
                copy_pT(3)
                if e1.exists():
                    act.wait_ge(outT_done, e1.nth(1, 1))
                    act.activation(flat(outT_hi), bank[2][:], ACT.Copy).then_inc(outT_hi_set, 1)

            slots(act, slot, {0: lambda: (upper_halves(K_W), upper_halves(V_W)),
                              1: lambda: (upper_halves(Q_W), upper_halves(C_W))})

        @block.vector
        def _(dve):
            dve.memset(ones[:], 1.0).then_inc(consts_set, 1)
            dve.memset(masked_bf[:], MASKED).then_inc(consts_set, 1)
            dve.memset(neghalf[:], -0.5).then_inc(consts_set, 1)
            dve.memset(mask_u8[:], 0).then_inc(consts_set, 1)
            dve.wait_ge(consts_set, 4)

            def prepare_small():
                dve.wait_ge(small_in, 16 * SMALL_DMAS)
                dve.tensor_scalar(q_scale[:], vecs[:, 0, :], SCALE, None, ALU.mult).then_inc(q_scale_set, 1)
                for n, i in enumerate((0, 1, 3)):
                    dve.wait_ge(small_turned, n + 1)
                    dve.tensor_copy(small_t[:, i, :], bank[n][:, 0:P]).then_inc(small_copied, 1)
                dve.wait_ge(wow_done, 1)
                dve.tensor_copy(small_t[:, 2, :], bank[3][:, 0:P]).then_inc(wow_copied, 1)
                dve.wait_ge(wow_done, 2)
                dve.tensor_tensor(out0_bias[:], bank[4][:, 0:1], bias0[:, 3:4], ALU.add).then_inc(wow_copied, 1)
                dve.wait_ge(wow_copied, 1)
                dve.wait_ge(small_copied, 3)
                dve.tensor_copy(small_hi[:], small_t[:, 0:3, :]).then_inc(small_hi_set, 1)
                dve.wait_ge(small_hi_set, 1)
                dve.tensor_tensor(small_lo[:], small_t[:, 0:3, :], small_hi[:].bitcast(F32),
                                  ALU.subtract).then_inc(small_lo_set, 1)
                for c in range(DC):
                    dve.tensor_scalar(vb_wide[:, c, :], ones[:], vecs[:, 4, c:c + 1], None,
                                      ALU.mult).then_inc(vb_wide_set, 1)

            def lower_halves(i):
                dve.wait_ge(stage_in[i % 2], 16 * (i // 2 + 1))
                if i == Q_W:
                    dve.wait_ge(q_scale_set, 1)
                for c in range(DC):
                    dve.wait_ge(w_hi_set, 4 * i + c + 1)
                    dve.scalar_tensor_tensor(out=qkvc_lo[:, i, c, :], in0=stage[:, i % 2, c, :],
                                             scalar=q_scale[:, c:c + 1] if i == Q_W else 1.0,
                                             in1=qkvc_hi[:, i, c, :].bitcast(F32), op0=ALU.mult,
                                             op1=ALU.subtract).then_inc(w_lo_set, 1)

            def prepare_q_and_cproj():
                lower_halves(Q_W)
                lower_halves(C_W)
                dve.wait_ge(q_bias_done, 1)
                dve.tensor_tensor(q_bias[:], bank[5][:, 0:DC], vecs[:, 2, :], ALU.add).then_inc(q_bias_set, 1)
                dve.wait_ge(q_bias_set, 1)
                dve.tensor_scalar(q_bias[:], q_bias[:], SCALE, None, ALU.mult).then_inc(q_bias_set, 1)
                dve.wait_ge(q_bias_set, 2)
                dve.wait_ge(attn_bias_done, 1)
                dve.tensor_copy(attn_bias[:], bank[6][:]).then_inc(attn_bias_set, 1)

            def lower(out, psum, hi, done):
                dve.tensor_tensor(out, psum, hi.bitcast(F32), ALU.subtract).then_inc(done, 1)

            def slot(s):
                e0, e1, e2, ahead = s, s + -1, s + -2, s + 1
                if e0.exists():
                    dve.wait_ge(ctxT_hi_set, e0.nth(1, 1))
                    lower(flat(ctxT_lo), bank[0][:], flat(ctxT_hi), ctxT_lo_set)
                    for i, b in enumerate((1, 3)):
                        dve.wait_ge(m_hi_set, e0.nth(2, i + 1))
                        dve.scalar_tensor_tensor(out=m_lo[:, i, :], in0=bank[b][:], scalar=bias0[:, i:i + 1],
                                                 in1=m_hi[:, i, :].bitcast(F32), op0=ALU.add,
                                                 op1=ALU.subtract).then_inc(m_lo_set, 1)
                if e1.exists():
                    dve.wait_ge(xnT_hi_set, e1.nth(1, 1))
                    lower(flat(xnT_lo), bank[4][:], flat(xnT_hi), xnT_lo_set)
                    dve.wait_ge(mask_loaded[e1.parity], e1.dma())
                    if e1.has_before(1):
                        dve.wait_ge(s1_done, (e1 + -1).nth(4, 4))
                    dve.tensor_scalar(mask_less_1[:], mask_u8[:, e1.parity, :], -1.0, None,
                                      ALU.add).then_inc(mask_set, 1)
                if ahead.exists():
                    u = ahead.parity
                    dve.wait_ge(x_loaded[u], ahead.dma())
                    dve.bn_stats(in_stats[:, 0, :], x_in[:, u, :]).then_inc(in_stat, 1)
                    dve.wait_ge(ctx_loaded[u], ahead.dma())
                    dve.bn_stats(in_stats[:, 1, :], ctx_in[:, u, :]).then_inc(in_stat, 1)
                    dve.wait_ge(in_stat, ahead.nth(2, 2))
                    dve.sem_inc(stats_seen, 1)
                    for i in range(2):
                        dve.bn_aggr(in_mv[:, i, :], in_stats[:, i, :]).then_inc(in_aggr, 1)
                    dve.wait_ge(in_aggr, ahead.nth(2, 2))
                    dve.tensor_scalar(in_ve[:], in_mv[:, :, 1], EPS, None, ALU.add).then_inc(in_veps, 1)
                if e2.exists():
                    dve.wait_ge(cproj_done, e2.nth(1, 1))
                    dve.wait_ge(x1b_set, e2.nth(1, 1))
                    if e2.has_before(2):
                        dve.wait_ge(hid_stored[e2.parity], (e2 + -2).dma())
                    dve.tensor_tensor(hid[:, e2.parity, :], bank[2][:], x1b[:, e2.parity, :],
                                      ALU.add).then_inc(hid_set, 1)

                def max0(t):
                    dve.wait_ge(s0_done, e0.nth(4, t + 1))
                    if t == 0 and e0.has_before(1):
                        dve.wait_ge(exp0_done, (e0 + -1).nth(4, 4))
                    dve.tensor_reduce(negmax0[:, t:t + 1], bank[S0_BANK[t]][:], AX_X, ALU.max,
                                      negate=True).then_inc(max0_set, 1)

                if e0.exists():
                    max0(0)
                    max0(1)
                if ahead.exists():
                    dve.wait_ge(in_rstd_ready, ahead.nth(1, 1))
                    if ahead.has_before(1):
                        dve.wait_ge(m_done, (ahead + -1).nth(2, 2))
                        dve.wait_ge(normed_lo_set, (ahead + -1).nth(2, 2))
                    for i, src in enumerate((x_in, ctx_in)):
                        dve.tensor_scalar(normed[:, i, :], src[:, ahead.parity, :], in_mv[:, i, 0:1], in_rstd[:, i:i + 1],
                                          ALU.subtract, ALU.mult).then_inc(normed_set, 1)
                    for i in range(2):
                        dve.wait_ge(normed_set, ahead.nth(2, i + 1))
                        dve.tensor_copy(normed_hi[:, i, :], normed[:, i, :]).then_inc(normed_hi_set, 1)
                if e0.exists():
                    max0(2)
                    max0(3)
                if e1.exists():
                    dve.wait_ge(qT_turned, e1.nth(1, 1))
                    dve.tensor_tensor(qT[:], by_chunk(3), q_bias[:].unsqueeze(2).to_broadcast([P, DC, P]),
                                      ALU.add).then_inc(qT_set, 1)

                def max1(r):
                    if e1.exists():
                        dve.wait_ge(s1_done, e1.nth(4, r + 1))
                        dve.tensor_reduce(negmax1[:, r, :], by_chunk(S1_BANK[r]), AX_X, ALU.max,
                                          negate=True).then_inc(max1_set, 1)

                def sum1_reciprocal(r):
                    if e1.exists():
                        dve.wait_ge(exp1_done, e1.nth(16, 4 * r + 4))
                        dve.reciprocal(rsum1[:, r, :], sum1[:, r, :]).then_inc(rsum1_set, 1)

                if e0.exists():
                    dve.wait_ge(exp0_done, e0.nth(4, 4))
                    dve.reciprocal(rsum0[:], sum0[:]).then_inc(rsum0_set, 1)
                    dve.wait_ge(rsum0_set, e0.nth(1, 1))
                    for t in range(DC):
                        dve.tensor_scalar(A[:, t, :], A[:, t, :], rsum0[:, t:t + 1], None,
                                          ALU.mult).then_inc(a_scaled, 1)

                def at_lower(j):
                    if e0.exists():
                        dve.wait_ge(at_hi_set, e0.nth(4, j + 1))
                        lower(at_lo[:, j, :], bank[AT_BANK[j]][:], at_hi[:, j, :], at_lo_set)

                max1(0)
                max1(1)
                sum1_reciprocal(0)
                if e0.exists():
                    dve.wait_ge(k_done, e0.nth(1, 1))
                    dve.tensor_copy(k_sb[:], bank[7][:]).then_inc(k_copied, 1)
                sum1_reciprocal(1)
                at_lower(0)
                max1(2)
                at_lower(1)
                max1(3)
                sum1_reciprocal(2)
                at_lower(2)
                at_lower(3)
                sum1_reciprocal(3)
                if e0.exists():
                    dve.wait_ge(u_hi_set, e0.nth(1, 1))
                    lower(u_lo[:], bank[7][:], u_hi[:], u_lo_set)
                    dve.wait_ge(kT_turned, e0.nth(1, 1))
                    dve.tensor_tensor(kT[:], by_chunk(0), vecs[:, 3, :].unsqueeze(2).to_broadcast([P, DC, P]),
                                      ALU.add).then_inc(kT_set, 1)
                if e0.exists():
                    dve.wait_ge(out0_done, e0.nth(1, 1))
                    if e0.has_before(1):
                        dve.wait_ge(x1b_set, (e0 + -1).nth(1, 1))
                    dve.scalar_tensor_tensor(out=x1[:], in0=bank[7][:], scalar=out0_bias[:, 0:1],
                                             in1=x_in[:, e0.parity, :], op0=ALU.add, op1=ALU.add)\
                       .then_inc(x1_set, 1)
                    dve.wait_ge(x1_set, e0.nth(1, 1))
                    dve.bn_stats(x1_stats[:], x1[:]).then_inc(x1_stat, 1)
                    dve.wait_ge(x1_stat, e0.nth(1, 1))
                    dve.sem_inc(stats_seen, 1)
                    dve.bn_aggr(x1_mv[:], x1_stats[:]).then_inc(x1_aggr, 1)
                    dve.wait_ge(x1_aggr, e0.nth(1, 1))
                    dve.tensor_scalar(x1_ve[:], x1_mv[:, 1:2], EPS, None, ALU.add).then_inc(x1_veps, 1)
                if e1.exists():
                    dve.wait_ge(outT_hi_set, e1.nth(1, 1))
                    lower(flat(outT_lo), bank[2][:], flat(outT_hi), outT_lo_set)
                if e0.exists():
                    dve.wait_ge(x1_rstd_ready, e0.nth(1, 1))
                    dve.tensor_scalar(x1n[:], x1[:], x1_mv[:, 0:1], x1_rstd[:, 0:1],
                                      ALU.subtract, ALU.mult).then_inc(x1n_set, 1)

            slots(dve, slot, {0: lambda: (prepare_small(), lower_halves(K_W), lower_halves(V_W)),
                              1: prepare_q_and_cproj})

        @block.tensor
        def _(pe):
            def three_passes(out, a_hi, a_lo, b_hi, b_lo, first=True, last=True):
                pe.matmul(out, a_hi, b_lo, start=first, stop=False)
                pe.matmul(out, a_lo, b_hi, start=False, stop=False)
                return pe.matmul(out, a_hi, b_hi, start=False, stop=last)

            def prepare_small():
                pe.wait_ge(small_in, 16 * SMALL_DMAS)
                pe.wait_ge(ident_set, 1)
                for n, i in enumerate((0, 1, 3)):
                    pe.transpose(bank[n][:, 0:P], small[:, i, :], ident[:]).then_inc(small_turned, 1)
                pe.wait_ge(small_copied, 3)
                pe.matmul(bank[3][:, 0:P], small[:, 2, :], small_t[:, 3, :], start=True, stop=True)\
                  .then_inc(wow_done, 1)
                pe.matmul(bank[4][:, 0:1], small_t[:, 3, :], bias0[:, 2:3], start=True, stop=True)\
                  .then_inc(wow_done, 1)
                pe.wait_ge(wow_copied, 2)
                pe.wait_ge(small_lo_set, 1)

            def prepare_biases():
                pe.wait_ge(stage_in[Q_W % 2], 32)
                for m in range(DC):
                    for c in range(DC):
                        last = pe.matmul(bank[5][:, m:m + 1], stage[:, Q_W % 2, c, m * P:(m + 1) * P],
                                         vecs[:, 1, c:c + 1], start=(c == 0), stop=(c == DC - 1))
                last.then_inc(q_bias_done, 1)
                pe.wait_ge(stage_in[C_W % 2], 32)
                pe.wait_ge(vb_wide_set, DC)
                for c in range(DC):
                    pe.matmul(bank[6][:], vb_wide[:, c, :], stage[:, C_W % 2, c, :], start=(c == 0), stop=False)
                pe.matmul(bank[6][:], ones[0:1, :], cb_row[:], start=False, stop=True).then_inc(attn_bias_done, 1)
                pe.wait_ge(w_lo_set, 16)
                pe.wait_ge(q_bias_set, 2)
                pe.wait_ge(attn_bias_set, 1)

            def turn(out, src, done):
                for c in range(DC):
                    last = pe.transpose(out[:, c * P:(c + 1) * P], src(c), ident[:])
                last.then_inc(done, 1)

            def project(out, hi, lo, weight, done, chunks=range(DC)):
                for c in chunks:
                    last = three_passes(out[:], hi[:, c, :], lo[:, c, :], qkvc_hi[:, weight, c, :],
                                        qkvc_lo[:, weight, c, :], c == 0, c == DC - 1)
                if c == DC - 1:
                    last.then_inc(done, 1)

            def slot(s):
                e0, e1, e2 = s, s + -1, s + -2

                if e0.exists():
                    if e1.exists():
                        pe.wait_ge(kT_set, e1.nth(1, 1))
                    pe.wait_ge(ctx_loaded[e0.parity], e0.dma())
                    turn(bank[0], lambda c: ctx_in[:, e0.parity, c * P:(c + 1) * P], ctxT_turned)
                    for i, b in enumerate((1, 3)):
                        pe.wait_ge(normed_lo_set, e0.nth(2, i + 1))
                        three_passes(bank[b][:], small_hi[:, i, :], small_lo[:, i, :], normed_hi[:, i, :],
                                     normed_lo[:, i, :]).then_inc(m_done, 1)
                if e2.exists():
                    pe.wait_ge(outT_lo_set, e2.nth(1, 1))
                    project(bank[2], outT_hi, outT_lo, C_W, cproj_done, range(0, 2))
                if e1.exists():
                    pe.wait_ge(x1n_set, e1.nth(1, 1))
                    turn(bank[4], lambda c: x1n[:, c * P:(c + 1) * P], xnT_turned)
                if e2.exists():
                    project(bank[2], outT_hi, outT_lo, C_W, cproj_done, range(2, 4))

                def scores0(t):
                    if e0.exists():
                        if t == 0:
                            pe.wait_ge(m_lo_set, e0.nth(2, 2))
                        if t == 2:
                            pe.wait_ge(ctxT_lo_set, e0.nth(1, 1))
                        cols = slice(t * P, (t + 1) * P)
                        three_passes(bank[S0_BANK[t]][:], m_hi[:, 0, cols], m_lo[:, 0, cols], m_hi[:, 1, :],
                                     m_lo[:, 1, :]).then_inc(s0_done, 1)

                scores0(0)
                scores0(1)
                if e1.exists():
                    pe.wait_ge(xnT_lo_set, e1.nth(1, 1))
                    project(bank[7], xnT_hi, xnT_lo, Q_W, q_done)
                scores0(2)
                scores0(3)
                if e1.exists():
                    pe.wait_ge(q_copied, e1.nth(1, 1))
                    turn(bank[3], lambda c: q_sb[:, c * P:(c + 1) * P], qT_turned)

                def scores1(r):
                    if r == 0 and e2.exists():
                        pe.wait_ge(hid_set, e2.nth(1, 1))
                    if r >= 2 and e0.exists():
                        pe.wait_ge(exp0_done, e0.nth(4, r - 1))
                    row = slice(32 * r, 32 * r + 1)
                    rows = slice(32 * r, 32 * r + 32)
                    if r == 0:
                        pe.wait_ge(mask_set, e1.nth(1, 1))
                        pe.wait_ge(kT_set, e1.nth(1, 1))
                        pe.wait_ge(qT_set, e1.nth(1, 1))
                    pe.matmul(by_chunk(S1_BANK[r]), masked_bf[row, :],
                              mask_less_1[row, :].unsqueeze(1).to_broadcast([1, 4, P]), start=True, stop=False)
                    for c in range(4):
                        mm = pe.matmul(bank[S1_BANK[r]][:, c * P:(c + 1) * P], qT[rows, c, :], kT[rows, c, :],
                                       start=False, stop=(c == 3))
                    mm.then_inc(s1_done, 1)

                if e0.exists():
                    if not e0.has_before(1):
                        pe.wait_ge(w_lo_set, 8)
                    project(bank[7], ctxT_hi, ctxT_lo, K_W, k_done, range(0, 2))
                if e1.exists():
                    scores1(0)
                if e0.exists():
                    project(bank[7], ctxT_hi, ctxT_lo, K_W, k_done, range(2, 4))
                if e1.exists():
                    scores1(1)
                if e0.exists():
                    pe.wait_ge(exp0_done, e0.nth(4, 3))
                    project(bank[0], ctxT_hi, ctxT_lo, V_W, v_done, range(0, 2))

                def turn_A(j):
                    if e0.exists():
                        if j == 0:
                            pe.wait_ge(a_scaled, e0.nth(4, 4))
                        if j >= 2 and e1.exists():
                            pe.wait_ge(exp1_done, e1.nth(16, 4 * (j - 1)))
                        turn(bank[AT_BANK[j]], lambda t: A[:, t, j * P:(j + 1) * P], at_turned)

                def values0(j):
                    if e0.exists():
                        if j == 0:
                            pe.wait_ge(k_copied, e0.nth(1, 1))
                        pe.wait_ge(at_lo_set, e0.nth(4, j + 1))
                        last = three_passes(bank[7][:], ctxT_hi[:, j, :], ctxT_lo[:, j, :], at_hi[:, j, :],
                                            at_lo[:, j, :], j == 0, j == DC - 1)
                        if j == DC - 1:
                            last.then_inc(u_done, 1)

                def turn_probs(r):
                    if e1.exists():
                        pe.wait_ge(exp1_done, e1.nth(16, 4 * r + 4))
                        pe.wait_ge(probs_set, e1.nth(4, r + 1))
                        turn(bank[PT_BANK[r]], lambda c: probs[:, r, c, :], pT_turned)

                turn_A(0)
                if e1.exists():
                    scores1(2)
                if e0.exists():
                    project(bank[0], ctxT_hi, ctxT_lo, V_W, v_done, range(2, 4))
                turn_A(1)
                if e1.exists():
                    scores1(3)
                turn_A(2)
                turn_A(3)
                values0(0)
                values0(1)
                turn_probs(0)
                values0(2)
                turn_probs(1)
                values0(3)
                turn_probs(2)
                turn_probs(3)
                if e0.exists():
                    pe.wait_ge(v_copied, e0.nth(1, 1))
                    pe.wait_ge(k_copied, e0.nth(1, 1))
                    turn(bank[0], lambda c: k_sb[:, c * P:(c + 1) * P], kT_turned)
                    pe.wait_ge(u_lo_set, e0.nth(1, 1))
                    three_passes(bank[7][:], small_hi[:, 2, :], small_lo[:, 2, :], u_hi[:], u_lo[:])\
                        .then_inc(out0_done, 1)
                if e1.exists():
                    pe.wait_ge(pT_copied, e1.nth(4, 4))
                    for c in range(4):
                        for r in range(4):
                            h = 4 * c + r
                            mm = pe.matmul(bank[2][32 * r:32 * r + 32, c * P:(c + 1) * P],
                                           v_sb[:, e1.parity, h * HD:(h + 1) * HD], pT[:, r, c, :],
                                           start=True, stop=True)
                    mm.then_inc(outT_done, 1)

            slots(pe, slot, {0: prepare_small, 1: prepare_biases})


def mlp_pass(nc, hidden, w, out, stage, mlp_staged):
    B, _, D = hidden.shape
    DC = D // P
    INNER = w["fc_w"].shape[1]
    IC = INNER // P
    TILES = 4
    N = TILES * P
    G = B // TILES
    STAGES = 2 * IC // STAGE
    assert B % TILES == 0 and DC == STAGE and IC % STAGE == 0

    with ExitStack() as stack:
        def sb(name, shape, dt=F32):
            return stack.enter_context(nc.sbuf_tensor(name, shape, dt))

        def sem(name):
            return stack.enter_context(nc.semaphore(name))

        acc = [stack.enter_context(nc.psum_tensor(f"acc{i}", [P, D], F32)) for i in range(TILES)]
        pre = [stack.enter_context(nc.psum_tensor(f"pre{i}", [P, N], F32)) for i in range(2)]
        tr = [stack.enter_context(nc.psum_tensor(f"tr{i}", [P, N], F32)) for i in range(2)]

        fc_hi = sb("fc_hi", [P, DC, INNER], F32R)
        fc_lo = sb("fc_lo", [P, DC, INNER], F32R)
        proj_hi = sb("proj_hi", [P, IC, D], F32R)
        proj_lo = sb("proj_lo", [P, IC, D], F32R)
        ln_vecs = sb("ln_vecs", [P, 2, DC])
        fc_bias = sb("fc_bias", [P, 2, IC])
        proj_bias = sb("proj_bias", [P, D])
        ident = sb("ident2", [P, P])
        neghalf = sb("neghalf2", [P, TILES])
        hid = sb("hid2", [P, 2, TILES, D])
        y = sb("y", [P, TILES, D])
        stats = sb("stats2", [P, TILES, 6])
        mv = sb("mv2", [P, TILES, 2])
        ve = sb("ve2", [P, TILES])
        rstd = sb("rstd2", [P, TILES])
        yT_hi = sb("yT_hi", [P, DC, N], F32R)
        yT_lo = sb("yT_lo", [P, DC, N], F32R)
        gl = sb("gl", [P, 2, N])
        hT_hi = sb("hT_hi", [P, 2, N], F32R)
        hT_lo = sb("hT_lo", [P, 2, N], F32R)

        vecs_in = sem("vecs_in")
        ident_zero = sem("ident_zero2")
        ident_set = sem("ident_set2")
        consts_set = sem("consts_set2")
        fc_b_done = sem("fc_b_done")
        fc_b_set = sem("fc_b_set")
        w_hi_set = sem("w_hi_set2")
        w_lo_set = sem("w_lo_set2")
        hid_loaded = [sem(f"hid_loaded{i}") for i in range(2)]
        out_stored = [sem(f"out_stored{i}") for i in range(2)]
        stat = sem("stat2")
        stats_seen = sem("stats_seen2")
        aggr = sem("aggr2")
        veps = sem("veps2")
        rstd_ready = sem("rstd_ready2")
        y_set = sem("y_set")
        bias_added = sem("bias_added")
        yT_turned = sem("yT_turned")
        yT_hi_set = sem("yT_hi_set")
        yT_lo_set = sem("yT_lo_set")
        fc_done = sem("fc_done")
        gelu_done = sem("gelu_done")
        hT_hi_set = sem("hT_hi_set")
        hT_lo_set = sem("hT_lo_set")
        proj_done = sem("proj_done")
        out_set = sem("out_set")

        PAIRS = (G - 2) // 2

        def groups(eng, group):
            group(Item(0, 0, G), True)
            with eng.Fori(0, PAIRS) as pair:
                for g in range(1, 3):
                    group(Item(pair, g, G), False)
            for g in range(1 + 2 * PAIRS, G):
                group(Item(0, g, G), False)

        def staged(eng, n):
            eng.wait_ge(mlp_staged[n % 2], 16 * (n // 2 + 1))

        def weight_block(fc, proj, n, c):
            if n % 2 == 0:
                return fc[:, c, (n // 2) * 512:(n // 2 + 1) * 512]
            return proj[:, STAGE * (n // 2) + c, :]

        def weight_scale(n, c):
            return ln_vecs[:, 0, c:c + 1] if n % 2 == 0 else 1.0

        block = stack.enter_context(nc.Block())

        @block.sync
        def _(sp):
            def load(g):
                if g.has_before(2):
                    sp.wait_ge(out_stored[g.parity], (g + -2).dma(TILES))
                sp.dma_start(hid[:, g.parity, :, :],
                             hidden[bass.ds(g.number * TILES, TILES)].rearrange("t p n -> p t n"))\
                  .then_inc(hid_loaded[g.parity], 16)

            load(Item(0, 0, G))
            for i, n in enumerate(("ln2_w", "ln2_b")):
                sp.dma_start(ln_vecs[:, i, :], w[n].rearrange("(c p) -> p c", p=P),
                             allow_slow_non_contiguous=True).then_inc(vecs_in, 16)
            sp.dma_start(fc_bias[:, 0, :], w["fc_b"].rearrange("(c p) -> p c", p=P),
                         allow_slow_non_contiguous=True).then_inc(vecs_in, 16)
            sp.dma_start(proj_bias[:], w["proj_b"].partition_broadcast(P)).then_inc(vecs_in, 16)
            load(Item(0, 1, G))
            for n in range(2, STAGES):
                sp.wait_ge(w_hi_set, STAGE * (n - 1))
                sp.wait_ge(w_lo_set, STAGE * (n - 1))
                if n % 2 == 0:
                    sp.wait_ge(fc_b_done, n // 2)
                sp.dma_start(stage[:, n % 2, :, :], mlp_stage_source(w, n)).then_inc(mlp_staged[n % 2], 16)

            def group(g, first):
                if (g + 1).exists() and not first:
                    load(g + 1)
                for t in range(TILES):
                    sp.wait_ge(out_set, g.nth(TILES, t + 1))
                    sp.dma_start(out[g.number * TILES + t], hid[:, g.parity, t, :])\
                      .then_inc(out_stored[g.parity], 16)

            groups(sp, group)
            for u in range(2):
                sp.wait_ge(out_stored[u], 16 * TILES * (G // 2))

        @block.gpsimd
        def _(pool):
            pool.memset(ident[:], 0.0).then_inc(ident_zero, 1)
            pool.wait_ge(ident_zero, 1)
            pool.affine_select(out=ident[:], in_=ident[:], compare_op=ALU.not_equal, fill=1.0, base=0,
                               pattern=[[-1, P]], channel_multiplier=1).then_inc(ident_set, 1)
            pool.wait_ge(consts_set, 1)

            def prepare(g):
                pool.wait_ge(veps, g.nth(1, 1))
                if g.has_before(1):
                    pool.wait_ge(y_set, (g + -1).nth(4, 4))
                pool.tensor_tensor(rstd[:], ve[:], neghalf[:], ALU.pow).then_inc(rstd_ready, 1)
                if not g.has_before(1):
                    pool.wait_ge(vecs_in, 16 * 4)
                for t in range(TILES):
                    pool.wait_ge(y_set, g.nth(4, t + 1))
                    pool.tensor_tensor(hid[:, g.parity, t, :], hid[:, g.parity, t, :], proj_bias[:],
                                       ALU.add).then_inc(bias_added, 1)

            prepare(Item(0, 0, G))

            def group(g, first):
                if (g + 1).exists():
                    prepare(g + 1)

            groups(pool, group)

        @block.scalar
        def _(act):
            def upper_halves(n):
                staged(act, n)
                for c in range(STAGE):
                    act.activation(weight_block(fc_hi, proj_hi, n, c), stage[:, n % 2, c, :], ACT.Identity,
                                   scale=weight_scale(n, c)).then_inc(w_hi_set, 1)

            def turned(g):
                for c in range(DC):
                    act.wait_ge(yT_turned, g.nth(4, c + 1))
                    act.activation(yT_hi[:, c, :], tr[c % 2][:], ACT.Copy).then_inc(yT_hi_set, 1)

            act.wait_ge(vecs_in, 16 * 4)
            upper_halves(0)
            turned(Item(0, 0, G))
            upper_halves(1)

            def group(g, first):
                for i in range(IC):
                    if first and i % STAGE == 0:
                        for n in range(i // STAGE * 2 + 2, min(i // STAGE * 2 + 4, STAGES)):
                            upper_halves(n)
                    if first:
                        act.wait_ge(fc_b_set, i // STAGE + 1)
                    act.wait_ge(fc_done, g.nth(IC, i + 1))
                    if i >= 2:
                        act.wait_ge(hT_lo_set, g.nth(IC, i - 1))
                    elif g.has_before(1):
                        act.wait_ge(hT_lo_set, (g + -1).nth(IC, IC - 1 + i))
                    act.activation(gl[:, i % 2, :], pre[i % 2][:], ACT.Gelu_apprx_tanh,
                                   bias=fc_bias[:, 1, i:i + 1]).then_inc(gelu_done, 1)
                if (g + 1).exists():
                    turned(g + 1)

            groups(act, group)

        @block.vector
        def _(dve):
            dve.memset(neghalf[:], -0.5).then_inc(consts_set, 1)

            def lower_halves(n):
                staged(dve, n)
                for c in range(STAGE):
                    dve.wait_ge(w_hi_set, STAGE * n + c + 1)
                    dve.scalar_tensor_tensor(out=weight_block(fc_lo, proj_lo, n, c), in0=stage[:, n % 2, c, :],
                                             scalar=weight_scale(n, c),
                                             in1=weight_block(fc_hi, proj_hi, n, c).bitcast(F32), op0=ALU.mult,
                                             op1=ALU.subtract).then_inc(w_lo_set, 1)

            def statistics(g, t):
                if t == 0:
                    dve.wait_ge(hid_loaded[g.parity], g.dma())
                dve.bn_stats(stats[:, t, :], hid[:, g.parity, t, :]).then_inc(stat, 1)
                if t == TILES - 1:
                    dve.wait_ge(stat, g.nth(4, 4))
                    dve.sem_inc(stats_seen, 1)
                    for i in range(TILES):
                        dve.bn_aggr(mv[:, i, :], stats[:, i, :]).then_inc(aggr, 1)
                    dve.wait_ge(aggr, g.nth(4, 4))
                    dve.tensor_scalar(ve[:], mv[:, :, 1], EPS, None, ALU.add).then_inc(veps, 1)

            def normalise(g, t):
                if t == 0:
                    dve.wait_ge(rstd_ready, g.nth(1, 1))
                    if g.has_before(1):
                        dve.wait_ge(yT_turned, (g + -1).nth(4, 4))
                dve.tensor_scalar(y[:, t, :], hid[:, g.parity, t, :], mv[:, t, 0:1], rstd[:, t:t + 1],
                                  ALU.subtract, ALU.mult).then_inc(y_set, 1)

            def turned(g):
                for c in range(DC):
                    dve.wait_ge(yT_hi_set, g.nth(4, c + 1))
                    dve.tensor_tensor(yT_lo[:, c, :], tr[c % 2][:], yT_hi[:, c, :].bitcast(F32),
                                      ALU.subtract).then_inc(yT_lo_set, 1)

            first_group = Item(0, 0, G)
            for t in range(TILES):
                statistics(first_group, t)
            for t in range(TILES):
                normalise(first_group, t)
            dve.wait_ge(vecs_in, 16 * 4)
            lower_halves(0)
            turned(first_group)
            lower_halves(1)

            def group(g, first):
                nxt = g + 1
                for i in range(IC):
                    if first and i % STAGE == 0:
                        k = i // STAGE
                        dve.wait_ge(fc_b_done, k + 1)
                        dve.tensor_tensor(fc_bias[:, 1, i:i + STAGE], tr[0][:, i:i + STAGE],
                                          fc_bias[:, 0, i:i + STAGE], ALU.add).then_inc(fc_b_set, 1)
                        for n in range(2 * k + 2, min(2 * k + 4, STAGES)):
                            lower_halves(n)
                    dve.wait_ge(gelu_done, g.nth(IC, i + 1))
                    if i >= 2:
                        dve.wait_ge(proj_done, g.nth(IC, i - 1))
                    elif g.has_before(1):
                        dve.wait_ge(proj_done, (g + -1).nth(IC, IC - 1 + i))
                    dve.tensor_copy(hT_hi[:, i % 2, :], gl[:, i % 2, :]).then_inc(hT_hi_set, 1)
                    dve.wait_ge(hT_hi_set, g.nth(IC, i + 1))
                    dve.tensor_tensor(hT_lo[:, i % 2, :], gl[:, i % 2, :], hT_hi[:, i % 2, :].bitcast(F32),
                                      ALU.subtract).then_inc(hT_lo_set, 1)
                    if nxt.exists():
                        if 3 <= i < 3 + TILES:
                            statistics(nxt, i - 3)
                        if 9 <= i < 9 + TILES:
                            normalise(nxt, i - 9)
                if nxt.exists():
                    turned(nxt)
                for t in range(TILES):
                    if t == 0:
                        dve.wait_ge(proj_done, g.nth(IC, IC))
                    dve.wait_ge(bias_added, g.nth(4, t + 1))
                    dve.tensor_tensor(hid[:, g.parity, t, :], acc[t][:], hid[:, g.parity, t, :],
                                      ALU.add).then_inc(out_set, 1)

            groups(dve, group)

        @block.tensor
        def _(pe):
            def turn(g, c):
                if c == 0:
                    pe.wait_ge(y_set, g.nth(4, 4))
                if c >= 2:
                    pe.wait_ge(yT_lo_set, g.nth(4, c - 1))
                elif g.has_before(1):
                    pe.wait_ge(yT_lo_set, (g + -1).nth(4, c + 3))
                for t in range(TILES):
                    last = pe.transpose(tr[c % 2][:, t * P:(t + 1) * P], y[:, t, c * P:(c + 1) * P], ident[:])
                last.then_inc(yT_turned, 1)

            def bias_products(k):
                if k == 0:
                    pe.wait_ge(vecs_in, 16 * 4)
                    pe.wait_ge(yT_lo_set, 4)
                staged(pe, 2 * k)
                for i in range(STAGE):
                    for c in range(DC):
                        last = pe.matmul(tr[0][:, k * STAGE + i:k * STAGE + i + 1],
                                         stage[:, 0, c, i * P:(i + 1) * P], ln_vecs[:, 1, c:c + 1],
                                         start=(c == 0), stop=(c == DC - 1))
                last.then_inc(fc_b_done, 1)

            def three_passes(out, a_hi, a_lo, b_hi, b_lo, first, last):
                pe.matmul(out, a_hi, b_lo, start=first, stop=False)
                pe.matmul(out, a_lo, b_hi, start=False, stop=False)
                return pe.matmul(out, a_hi, b_hi, start=False, stop=last)

            def fc(g, i):
                if i == 0:
                    pe.wait_ge(yT_lo_set, g.nth(4, 4))
                if i >= 2:
                    pe.wait_ge(gelu_done, g.nth(IC, i - 1))
                elif g.has_before(1):
                    pe.wait_ge(gelu_done, (g + -1).nth(IC, IC - 1 + i))
                cols = slice(i * P, (i + 1) * P)
                for c in range(DC):
                    last = three_passes(pre[i % 2][:], fc_hi[:, c, cols], fc_lo[:, c, cols], yT_hi[:, c, :],
                                        yT_lo[:, c, :], c == 0, c == DC - 1)
                last.then_inc(fc_done, 1)

            def proj(g, i):
                pe.wait_ge(hT_lo_set, g.nth(IC, i + 1))
                if i == 0 and g.has_before(1):
                    pe.wait_ge(out_set, (g + -1).nth(4, 4))
                for t in range(TILES):
                    cols = slice(t * P, (t + 1) * P)
                    last = three_passes(acc[t][:], hT_hi[:, i % 2, cols], hT_lo[:, i % 2, cols], proj_hi[:, i, :],
                                        proj_lo[:, i, :], i == 0, i == IC - 1)
                last.then_inc(proj_done, 1)

            pe.wait_ge(ident_set, 1)
            for c in range(DC):
                turn(Item(0, 0, G), c)

            def group(g, first):
                more = (g + 1).exists()
                for i in range(IC):
                    if first and i % STAGE == 0:
                        bias_products(i // STAGE)
                        pe.wait_ge(w_lo_set, STAGE * (i // STAGE * 2 + 2))
                    fc(g, i)
                    if i == IC - 1 and more:
                        if first:
                            pe.wait_ge(fc_b_set, IC // STAGE)
                        turn(g + 1, 0)
                        turn(g + 1, 1)
                    if i >= 1:
                        proj(g, i - 1)
                if more:
                    turn(g + 1, 2)
                    turn(g + 1, 3)
                proj(g, IC - 1)

            groups(pe, group)


def kernel(**inputs):
    import numpy as np
    import concourse.bacc as bacc
    from concourse.bass_utils import run_bass_kernel_spmd

    nc = bacc.Bacc("TRN2", target_bir_lowering=False, num_devices=1)
    arrays, aps = {}, {}
    for name, value in inputs.items():
        a = np.ascontiguousarray(value)
        if a.dtype == np.bool_:
            a = a.view(np.uint8)
        arrays[f"in_{name}"] = a
        aps[name] = nc.dram_tensor(f"in_{name}", a.shape, mybir.dt.from_np(a.dtype), kind="ExternalInput").ap()
    shape = inputs["x"].shape
    out = nc.dram_tensor("out", shape, F32, kind="ExternalOutput").ap()
    hidden = nc.dram_tensor("hidden", shape, F32, kind="Internal").ap()
    w = {name.split("_xattn_", 1)[1]: ap for name, ap in aps.items() if "_xattn_" in name}
    with nc.sbuf_tensor("stage", [P, 2, STAGE, 512], F32) as stage, \
            nc.semaphore("mlp_staged0") as staged0, nc.semaphore("mlp_staged1") as staged1:
        attention_pass(nc, aps["x"], aps["ctx_2048"], aps["mask_BxS2_bf1"], w, hidden, stage, (staged0, staged1))
        mlp_pass(nc, hidden, w, out, stage, (staged0, staged1))
    r = run_bass_kernel_spmd(nc, [arrays], core_ids=[0])
    return r.results[0]["out"]
```

```python
from contextlib import ExitStack

import concourse.bass as bass
from concourse import mybir

F32 = mybir.dt.float32
F32R = mybir.dt.float32r
BF16 = mybir.dt.bfloat16
U8 = mybir.dt.uint8
ALU = mybir.AluOpType
ACT = mybir.ActivationFunctionType
AX_X = mybir.AxisListType.X

P = 128
EPS = 1e-5
HEADS = 16
STAGE = 4
TILES = 4
MASKED = 3.3895313892515355e38


class Item:

    def __init__(self, pair, offset, count):
        self.pair, self.offset, self.count = pair, offset, count

    def __add__(self, k):
        return Item(self.pair, self.offset + k, self.count)

    def exists(self):
        return not isinstance(self.pair, int) or 0 <= self.offset < self.count

    def has_before(self, k=1):
        return not isinstance(self.pair, int) or self.offset - k >= 0

    @property
    def parity(self):
        return self.offset % 2

    @property
    def number(self):
        return self.pair * 2 + self.offset

    def nth(self, per_item, k):
        return self.pair * (2 * per_item) + (self.offset * per_item + k)

    def dma(self, k=1):
        return self.pair * (16 * k) + (self.offset // 2 + 1) * (16 * k)


def mlp_stage_source(w, n):
    if n % 2 == 0:
        return w["fc_w"].rearrange("(c p) n -> p c n", p=P)[:, :, (n // 2) * 512:(n // 2 + 1) * 512]
    return w["proj_w"].rearrange("(c p) n -> p c n", p=P)[:, STAGE * (n // 2):STAGE * (n // 2 + 1), :]


class Handover:

    def __init__(self, nc, stack):
        def sb(name, shape, dt=F32):
            return stack.enter_context(nc.sbuf_tensor(name, shape, dt))

        def sem(name):
            return stack.enter_context(nc.semaphore(name))

        self.ident = sb("ident", [P, P])
        self.neghalf = sb("neghalf", [P, TILES])
        self.stage = sb("stage", [P, 2, STAGE, 512])
        self.rows = sb("rows", [P, 2, TILES, 512])
        self.y = sb("y", [P, TILES, 512])
        self.first_hi = sb("first_hi", [P, 2, STAGE, 512], F32R)
        self.first_lo = sb("first_lo", [P, 2, STAGE, 512], F32R)
        self.hid = sb("hid", [P, 2, 512])
        self.ln_vecs = sb("ln_vecs", [P, 2, 4])
        self.fc_bias = sb("fc_bias", [P, 16])
        self.stats = sb("stats", [P, TILES, 6])
        self.mv = sb("mv", [P, TILES, 2])
        self.ve = sb("ve", [P, TILES])
        self.rstd = sb("rstd", [P, TILES])
        self.hid_stored = [sem(f"hid_stored{i}") for i in range(2)]
        self.w_hi_set = sem("mlp_w_hi_set")
        self.w_lo_set = sem("mlp_w_lo_set")
        self.staged = [sem(f"mlp_staged{i}") for i in range(2)]
        self.vecs_in = sem("mlp_vecs_in")
        self.rows_loaded = [sem(f"rows_loaded{i}") for i in range(2)]
        self.stat = sem("mlp_stat")
        self.stats_seen = sem("mlp_stats_seen")
        self.aggr = sem("mlp_aggr")
        self.veps = sem("mlp_veps")
        self.rstd_ready = sem("mlp_rstd_ready")
        self.y_set = sem("mlp_y_set")

    def upper_half(self, act, out, n, c):
        if c == 0:
            act.wait_ge(self.staged[n % 2], 16 * (n // 2 + 1))
        act.activation(out, self.stage[:, n % 2, c, :], ACT.Copy).then_inc(self.w_hi_set, 1)

    def lower_half(self, dve, out, hi, n, c):
        if c == 0:
            dve.wait_ge(self.staged[n % 2], 16 * (n // 2 + 1))
        dve.wait_ge(self.w_hi_set, STAGE * n + c + 1)
        dve.tensor_tensor(out, self.stage[:, n % 2, c, :], hi.bitcast(F32), ALU.subtract)\
           .then_inc(self.w_lo_set, 1)

    def load_rows(self, sp, hidden, g):
        sp.dma_start(self.rows[:, g.parity, :, :],
                     hidden[bass.ds(g.number * TILES, TILES)].rearrange("t p n -> p t n"))\
          .then_inc(self.rows_loaded[g.parity], 16)

    def statistics(self, dve, g, t):
        if t == 0:
            dve.wait_ge(self.rows_loaded[g.parity], g.dma())
        dve.bn_stats(self.stats[:, t, :], self.rows[:, g.parity, t, :]).then_inc(self.stat, 1)
        if t == TILES - 1:
            dve.wait_ge(self.stat, g.nth(4, 4))
            dve.sem_inc(self.stats_seen, 1)
            for i in range(TILES):
                dve.bn_aggr(self.mv[:, i, :], self.stats[:, i, :]).then_inc(self.aggr, 1)
            dve.wait_ge(self.aggr, g.nth(4, 4))
            dve.tensor_scalar(self.ve[:], self.mv[:, :, 1], EPS, None, ALU.add).then_inc(self.veps, 1)

    def inverse_deviations(self, pool, g):
        pool.wait_ge(self.veps, g.nth(1, 1))
        if g.has_before(1):
            pool.wait_ge(self.y_set, (g + -1).nth(4, 4))
        pool.tensor_tensor(self.rstd[:], self.ve[:], self.neghalf[:], ALU.pow).then_inc(self.rstd_ready, 1)

    def normalise(self, dve, g, t):
        if t == 0:
            dve.wait_ge(self.rstd_ready, g.nth(1, 1))
        dve.tensor_scalar(self.y[:, t, :], self.rows[:, g.parity, t, :], self.mv[:, t, 0:1],
                          self.rstd[:, t:t + 1], ALU.subtract, ALU.mult).then_inc(self.y_set, 1)


def attention_pass(nc, x, ctx, mask, w, hidden, mlp):
    B, C, T = x.shape
    D = T
    DC = D // P
    HD = D // HEADS
    SCALE = float(HD) ** -0.5
    assert C == P and D == 4 * P and HD == 32

    with ExitStack() as stack:
        def sb(name, shape, dt=F32):
            return stack.enter_context(nc.sbuf_tensor(name, shape, dt))

        def sem(name):
            return stack.enter_context(nc.semaphore(name))

        bank = [stack.enter_context(nc.psum_tensor(f"bank{i}", [P, 512], F32)) for i in range(8)]

        ident, neghalf, stage = mlp.ident, mlp.neghalf, mlp.stage
        hid, hid_stored = mlp.hid, mlp.hid_stored
        A = mlp.rows[:, 0, :, :]
        probs = mlp.rows[:, 1, :, :].rearrange("p r (c n) -> p r c n", n=P)
        pT = mlp.y[:].rearrange("p r (c n) -> p r c n", n=P)

        qc_hi = sb("qc_hi", [P, 2, DC, D], F32R)
        qc_lo = sb("qc_lo", [P, 2, DC, D], F32R)
        small = sb("small", [P, 4, P])
        small_t = sb("small_t", [P, 4, P])
        small_hi = sb("small_hi", [P, 3, P], F32R)
        small_lo = sb("small_lo", [P, 3, P], F32R)
        vecs = sb("vecs", [P, 4, DC])
        q_scale = sb("q_scale", [P, DC])
        bias0 = sb("bias0", [P, 4])
        out0_bias = sb("out0_bias", [P, 1])
        q_bias = sb("q_bias", [P, DC])
        v_bias = sb("v_bias", [P, D])
        cproj_bias = sb("cproj_bias", [P, D])
        masked_bf = sb("masked_bf", [P, P], BF16)

        x_in = sb("x_in", [P, 2, T])
        ctx_in = sb("ctx_in", [P, 2, T])
        in_stats = sb("in_stats", [P, 2, 6])
        in_mv = sb("in_mv", [P, 2, 2])
        in_ve = sb("in_ve", [P, 2])
        in_rstd = sb("in_rstd", [P, 2])
        normed = sb("normed", [P, 2, T])
        normed_hi = sb("normed_hi", [P, 2, T], F32R)
        normed_lo = sb("normed_lo", [P, 2, T], F32R)
        m_hi = sb("m_hi", [P, 2, T], F32R)
        m_lo = sb("m_lo", [P, 2, T], F32R)
        ctxT_hi = sb("ctxT_hi", [P, DC, P], F32R)
        ctxT_lo = sb("ctxT_lo", [P, DC, P], F32R)
        negmax0 = sb("negmax0", [P, DC])
        sum0 = sb("sum0", [P, DC])
        rsum0 = sb("rsum0", [P, DC])
        at_hi = sb("at_hi", [P, DC, T], F32R)
        at_lo = sb("at_lo", [P, DC, T], F32R)
        u_hi = sb("u_hi", [P, T], F32R)
        u_lo = sb("u_lo", [P, T], F32R)
        x1 = sb("x1", [P, D])
        x1_stats = sb("x1_stats", [P, 6])
        x1_mv = sb("x1_mv", [P, 2])
        x1_ve = sb("x1_ve", [P, 1])
        x1_rstd = sb("x1_rstd", [P, 1])
        x1b = sb("x1b", [P, 2, D])
        x1n = sb("x1n", [P, D])
        xnT_hi = sb("xnT_hi", [P, DC, P], F32R)
        xnT_lo = sb("xnT_lo", [P, DC, P], F32R)
        q_sb = sb("q_sb", [P, D])
        k_sb = sb("k_sb", [P, D])
        qT = sb("qT", [P, DC, P])
        kT = sb("kT", [P, DC, P])
        v_sb = sb("v_sb", [P, 2, D])
        mask_u8 = sb("mask_u8", [P, 2, P], U8)
        mask_less_1 = sb("mask_less_1", [P, P], BF16)
        negmax1 = sb("negmax1", [P, 4, 4])
        sum1 = sb("sum1", [P, 4, 4])
        rsum1 = sb("rsum1", [P, 4, 4])
        outT_hi = sb("outT_hi", [P, DC, P], F32R)
        outT_lo = sb("outT_lo", [P, DC, P], F32R)

        sp_steps = sem("sp_steps")
        small_in = sem("small_in")
        vecs_in = sem("vecs_in")
        stage_in = [sem(f"stage_in{i}") for i in range(2)]
        consts_set = sem("consts_set")
        ident_zero = sem("ident_zero")
        ident_set = sem("ident_set")
        small_turned = sem("small_turned")
        small_copied = sem("small_copied")
        wow_done = sem("wow_done")
        wow_copied = sem("wow_copied")
        small_hi_set = sem("small_hi_set")
        small_lo_set = sem("small_lo_set")
        q_scale_set = sem("q_scale_set")
        q_bias_done = sem("q_bias_done")
        q_bias_set = sem("q_bias_set")
        w_hi_set = sem("w_hi_set")
        w_lo_set = [sem(f"w_lo_set{i}") for i in range(4)]
        x_loaded = [sem(f"x_loaded{i}") for i in range(2)]
        ctx_loaded = [sem(f"ctx_loaded{i}") for i in range(2)]
        mask_loaded = [sem(f"mask_loaded{i}") for i in range(2)]
        in_stat = sem("in_stat")
        stats_seen = sem("stats_seen")
        in_aggr = sem("in_aggr")
        in_veps = sem("in_veps")
        in_rstd_ready = sem("in_rstd_ready")
        normed_set = sem("normed_set")
        normed_hi_set = sem("normed_hi_set")
        normed_lo_set = sem("normed_lo_set")
        ctxT_turned = sem("ctxT_turned")
        ctxT_hi_set = sem("ctxT_hi_set")
        ctxT_lo_set = sem("ctxT_lo_set")
        m_done = sem("m_done")
        m_hi_set = sem("m_hi_set")
        m_lo_set = sem("m_lo_set")
        s0_done = sem("s0_done")
        max0_set = sem("max0_set")
        exp0_done = sem("exp0_done")
        rsum0_set = sem("rsum0_set")
        a_scaled = sem("a_scaled")
        at_turned = sem("at_turned")
        at_hi_set = sem("at_hi_set")
        at_lo_set = sem("at_lo_set")
        u_done = sem("u_done")
        u_hi_set = sem("u_hi_set")
        u_lo_set = sem("u_lo_set")
        out0_done = sem("out0_done")
        x1_set = sem("x1_set")
        x1_stat = sem("x1_stat")
        x1_aggr = sem("x1_aggr")
        x1_veps = sem("x1_veps")
        x1_rstd_ready = sem("x1_rstd_ready")
        x1n_set = sem("x1n_set")
        x1b_set = sem("x1b_set")
        xnT_turned = sem("xnT_turned")
        xnT_hi_set = sem("xnT_hi_set")
        xnT_lo_set = sem("xnT_lo_set")
        q_done = sem("q_done")
        q_copied = sem("q_copied")
        qT_turned = sem("qT_turned")
        qT_set = sem("qT_set")
        k_done = sem("k_done")
        k_copied = sem("k_copied")
        kT_turned = sem("kT_turned")
        kT_set = sem("kT_set")
        v_done = sem("v_done")
        v_set = sem("v_set")
        mask_set = sem("mask_set")
        s1_done = sem("s1_done")
        max1_set = sem("max1_set")
        exp1_done = sem("exp1_done")
        rsum1_set = sem("rsum1_set")
        probs_set = sem("probs_set")
        pT_turned = sem("pT_turned")
        pT_copied = sem("pT_copied")
        outT_done = sem("outT_done")
        outT_hi_set = sem("outT_hi_set")
        outT_lo_set = sem("outT_lo_set")
        cproj_done = sem("cproj_done")
        hid_set = sem("hid_set")

        WEIGHTS = ("k_w", "v_w", "q_w", "cproj_w")
        K_W, V_W, Q_W, C_W = range(4)

        def weight_hi(i, c):
            return mlp.first_hi[:, i, c, :] if i < 2 else qc_hi[:, i - 2, c, :]

        def weight_lo(i, c):
            return mlp.first_lo[:, i, c, :] if i < 2 else qc_lo[:, i - 2, c, :]

        S0_BANK = (5, 6, 0, 1)
        S1_BANK = (2, 4, 5, 6)
        AT_BANK = (1, 3, 2, 4)
        PT_BANK = (1, 3, 5, 6)

        FIRST, LOOPED, LAST = -1, 3, B + 1
        PAIRS = (B - 1 - LOOPED) // 2

        def slots(eng, slot, ahead=None):
            for s in range(FIRST, LOOPED):
                if ahead and s in ahead:
                    ahead[s]()
                slot(Item(0, s, B))
            with eng.Fori(0, PAIRS) as pair:
                for s in range(LOOPED, LOOPED + 2):
                    slot(Item(pair, s, B))
            for s in range(LOOPED + 2 * PAIRS, LAST + 1):
                if ahead and s in ahead:
                    ahead[s]()
                slot(Item(0, s, B))

        def flat(t):
            return t[:].rearrange("p c n -> p (c n)")

        def by_chunk(b):
            return bank[b][:].rearrange("p (c n) -> p c n", n=P)

        block = stack.enter_context(nc.Block())

        @block.sync
        def _(sp):
            def after(semaphore, value):
                sp.wait_ge(semaphore, value)
                sp.sem_inc(sp_steps, 1)

            def load(e):
                if e.has_before(2):
                    after(x1_set, (e + -2).nth(1, 1))
                    after(ctxT_turned, (e + -2).nth(1, 1))
                    after(normed_set, (e + -2).nth(2, 2))
                u = e.parity
                sp.dma_start(x_in[:, u, :], x[e.number]).then_inc(x_loaded[u], 16)
                sp.dma_start(ctx_in[:, u, :], ctx[e.number]).then_inc(ctx_loaded[u], 16)

            def stage_weight(i):
                if i >= 2:
                    sp.wait_ge(w_hi_set, 4 * (i - 1))
                    sp.wait_ge(w_lo_set[i - 2], 4)
                sp.dma_start(stage[:, i % 2, :, :],
                             w[WEIGHTS[i]].rearrange("(c p) n -> p c n", p=P)).then_inc(stage_in[i % 2], 16)

            load(Item(0, 0, B))
            for i, n in enumerate(("Wn", "Wm", "Wl", "Wo")):
                sp.dma_start(small[:, i, :], w[n]).then_inc(small_in, 16)
            for i, n in enumerate(("bn", "bm", "bl", "bo")):
                sp.dma_start(bias0[:, i:i + 1], w[n].rearrange("(p a) -> p a", a=1)).then_inc(small_in, 16)
            stage_weight(0)
            stage_weight(1)
            for i, n in enumerate(("ln1_w", "ln1_b", "q_b", "k_b")):
                sp.dma_start(vecs[:, i, :], w[n].rearrange("(c p) -> p c", p=P),
                             allow_slow_non_contiguous=True).then_inc(vecs_in, 16)
            sp.dma_start(v_bias[:], w["v_b"].partition_broadcast(P)).then_inc(vecs_in, 16)
            sp.dma_start(cproj_bias[:], w["cproj_b"].partition_broadcast(P)).then_inc(vecs_in, 16)
            load(Item(0, 1, B))
            stage_weight(2)
            stage_weight(3)

            def slot(s):
                e = s + 1
                if e.exists() and e.has_before(2):
                    load(e)
                e = s + -1
                if e.exists():
                    u = e.parity
                    if e.has_before(2):
                        after(mask_set, (e + -2).nth(1, 1))
                    else:
                        sp.wait_ge(consts_set, 3)
                    sp.dma_start(mask_u8[0:P:32, u, :],
                                 mask[e.number].partition_broadcast(4)).then_inc(mask_loaded[u], 16)
                e = s + -2
                if e.exists():
                    after(hid_set, e.nth(1, 1))
                    sp.dma_start(hidden[e.number], hid[:, e.parity, :]).then_inc(hid_stored[e.parity], 16)

            def load_for_mlp():
                sp.wait_ge(w_hi_set, 16)
                for i in range(4):
                    sp.wait_ge(w_lo_set[i], 4)
                for u in range(2):
                    sp.wait_ge(hid_stored[u], 16 * (TILES // 2))
                sp.wait_ge(at_turned, 4 * B)
                mlp.load_rows(sp, hidden, Item(0, 0, 1))
                for i, n in enumerate(("ln2_w", "ln2_b")):
                    sp.dma_start(mlp.ln_vecs[:, i, :], w[n].rearrange("(c p) -> p c", p=P),
                                 allow_slow_non_contiguous=True).then_inc(mlp.vecs_in, 16)
                sp.dma_start(mlp.fc_bias[:], w["fc_b"].rearrange("(c p) -> p c", p=P),
                             allow_slow_non_contiguous=True).then_inc(mlp.vecs_in, 16)
                for n in range(2):
                    sp.dma_start(stage[:, n, :, :], mlp_stage_source(w, n)).then_inc(mlp.staged[n], 16)

            slots(sp, slot, {B: load_for_mlp})

        @block.gpsimd
        def _(pool):
            pool.memset(ident[:], 0.0).then_inc(ident_zero, 1)
            pool.wait_ge(ident_zero, 1)
            pool.affine_select(out=ident[:], in_=ident[:], compare_op=ALU.not_equal, fill=1.0, base=0,
                               pattern=[[-1, P]], channel_multiplier=1).then_inc(ident_set, 1)
            pool.wait_ge(consts_set, 3)

            def lower_halves(i):
                pool.wait_ge(stage_in[i % 2], 16 * (i // 2 + 1))
                for c in range(DC):
                    pool.wait_ge(w_hi_set, 4 * i + c + 1)
                    pool.tensor_tensor(weight_lo(i, c), stage[:, i % 2, c, :], weight_hi(i, c).bitcast(F32),
                                       ALU.subtract).then_inc(w_lo_set[i], 1)

            def slot(s):
                e = s + -1
                if e.exists():
                    pool.wait_ge(x1_set, e.nth(1, 1))
                    if e.has_before(2):
                        pool.wait_ge(hid_set, (e + -2).nth(1, 1))
                    else:
                        pool.wait_ge(vecs_in, 16 * 6)
                    pool.tensor_tensor(x1b[:, e.parity, :], x1[:], cproj_bias[:], ALU.add).then_inc(x1b_set, 1)
                e = s + 1
                if e.exists():
                    pool.wait_ge(in_veps, e.nth(1, 1))
                    if e.has_before(1):
                        pool.wait_ge(normed_set, (e + -1).nth(2, 2))
                    pool.tensor_tensor(in_rstd[:], in_ve[:], neghalf[:, 0:2], ALU.pow).then_inc(in_rstd_ready, 1)
                    for i in range(2):
                        pool.wait_ge(normed_hi_set, e.nth(2, i + 1))
                        if e.has_before(1):
                            pool.wait_ge(m_done, (e + -1).nth(2, 2))
                        pool.tensor_tensor(normed_lo[:, i, :], normed[:, i, :], normed_hi[:, i, :].bitcast(F32),
                                           ALU.subtract).then_inc(normed_lo_set, 1)
                e = s + -1
                if e.exists():
                    if not e.has_before(1):
                        lower_halves(C_W)
                    for r in range(4):
                        pool.wait_ge(rsum1_set, e.nth(4, r + 1))
                        pool.tensor_tensor(probs[:, r, :, :], probs[:, r, :, :],
                                           rsum1[:, r, :].unsqueeze(2).to_broadcast([P, 4, P]),
                                           ALU.mult).then_inc(probs_set, 1)
                e = s
                if e.exists():
                    pool.wait_ge(x1_veps, e.nth(1, 1))
                    if e.has_before(1):
                        pool.wait_ge(x1n_set, (e + -1).nth(1, 1))
                    pool.tensor_tensor(x1_rstd[:], x1_ve[:], neghalf[:, 0:1], ALU.pow).then_inc(x1_rstd_ready, 1)

            def first_group():
                mlp.inverse_deviations(pool, Item(0, 0, 1))
                for c in range(STAGE):
                    mlp.lower_half(pool, mlp.first_lo[:, 1, c, :], mlp.first_hi[:, 1, c, :], 1, c)

            slots(pool, slot, {0: lambda: lower_halves(V_W), LAST: first_group})

        @block.scalar
        def _(act):
            act.wait_ge(small_in, 16 * 8)

            def upper_halves(i):
                act.wait_ge(stage_in[i % 2], 16 * (i // 2 + 1))
                if i == Q_W:
                    act.wait_ge(q_scale_set, 1)
                for c in range(DC):
                    act.activation(weight_hi(i, c), stage[:, i % 2, c, :], ACT.Identity,
                                   scale=q_scale[:, c:c + 1] if i == Q_W else 1.0).then_inc(w_hi_set, 1)

            def slot(s):
                e0, e1 = s, s + -1
                if e0.exists():
                    act.wait_ge(ctxT_turned, e0.nth(1, 1))
                    act.activation(flat(ctxT_hi), bank[0][:], ACT.Copy).then_inc(ctxT_hi_set, 1)
                    for i, b in enumerate((1, 3)):
                        act.wait_ge(m_done, e0.nth(2, i + 1))
                        act.activation(m_hi[:, i, :], bank[b][:], ACT.Identity,
                                       bias=bias0[:, i:i + 1]).then_inc(m_hi_set, 1)
                if e1.exists():
                    act.wait_ge(xnT_turned, e1.nth(1, 1))
                    act.activation(flat(xnT_hi), bank[4][:], ACT.Copy).then_inc(xnT_hi_set, 1)

                def exp0(t):
                    if e0.exists():
                        act.wait_ge(max0_set, e0.nth(4, t + 1))
                        act.activation(A[:, t, :], bank[S0_BANK[t]][:], ACT.Exp, bias=negmax0[:, t:t + 1],
                                       accum_out=sum0[:, t:t + 1]).then_inc(exp0_done, 1)

                exp0(0)
                if e1.exists():
                    act.wait_ge(q_done, e1.nth(1, 1))
                    act.activation(q_sb[:], bank[7][:], ACT.Copy).then_inc(q_copied, 1)
                exp0(1)
                exp0(2)
                exp0(3)

                def exp1(r):
                    if e1.exists():
                        act.wait_ge(max1_set, e1.nth(4, r + 1))
                        if e1.has_before(1):
                            act.wait_ge(pT_turned, (e1 + -1).nth(4, r + 1))
                        for c in range(4):
                            act.activation(probs[:, r, c, :], by_chunk(S1_BANK[r])[:, c, :], ACT.Exp,
                                           bias=negmax1[:, r, c:c + 1],
                                           accum_out=sum1[:, r, c:c + 1]).then_inc(exp1_done, 1)

                def at_upper(j):
                    if e0.exists():
                        act.wait_ge(at_turned, e0.nth(4, j + 1))
                        act.activation(at_hi[:, j, :], bank[AT_BANK[j]][:], ACT.Copy).then_inc(at_hi_set, 1)

                def copy_pT(r):
                    if e1.exists():
                        act.wait_ge(pT_turned, e1.nth(4, r + 1))
                        act.activation(pT[:, r, :, :].rearrange("p c n -> p (c n)"), bank[PT_BANK[r]][:],
                                       ACT.Copy).then_inc(pT_copied, 1)

                if e1.exists() and not e1.has_before(1):
                    upper_halves(C_W)
                exp1(0)
                at_upper(0)
                exp1(1)
                at_upper(1)
                at_upper(2)
                exp1(2)
                at_upper(3)
                exp1(3)
                copy_pT(0)
                if e0.exists():
                    act.wait_ge(u_done, e0.nth(1, 1))
                    act.activation(u_hi[:], bank[7][:], ACT.Copy).then_inc(u_hi_set, 1)
                copy_pT(1)
                copy_pT(2)
                copy_pT(3)
                if e1.exists():
                    act.wait_ge(outT_done, e1.nth(1, 1))
                    act.activation(flat(outT_hi), bank[2][:], ACT.Copy).then_inc(outT_hi_set, 1)

            def first_weights():
                act.wait_ge(k_done, B)
                act.wait_ge(v_done, B)
                for n in range(2):
                    for c in range(STAGE):
                        mlp.upper_half(act, mlp.first_hi[:, n, c, :], n, c)

            slots(act, slot, {0: lambda: (upper_halves(K_W), upper_halves(V_W)),
                              1: lambda: upper_halves(Q_W),
                              LAST: first_weights})

        @block.vector
        def _(dve):
            dve.memset(masked_bf[:], MASKED).then_inc(consts_set, 1)
            dve.memset(neghalf[:], -0.5).then_inc(consts_set, 1)
            dve.memset(mask_u8[:], 0).then_inc(consts_set, 1)
            dve.wait_ge(consts_set, 3)

            def prepare_small():
                dve.wait_ge(small_in, 16 * 8)
                for n, i in enumerate((0, 1, 3)):
                    dve.wait_ge(small_turned, n + 1)
                    dve.tensor_copy(small_t[:, i, :], bank[n][:, 0:P]).then_inc(small_copied, 1)
                dve.wait_ge(wow_done, 1)
                dve.tensor_copy(small_t[:, 2, :], bank[3][:, 0:P]).then_inc(wow_copied, 1)
                dve.wait_ge(wow_done, 2)
                dve.tensor_tensor(out0_bias[:], bank[4][:, 0:1], bias0[:, 3:4], ALU.add).then_inc(wow_copied, 1)
                dve.wait_ge(wow_copied, 1)
                dve.wait_ge(small_copied, 3)
                dve.tensor_copy(small_hi[:], small_t[:, 0:3, :]).then_inc(small_hi_set, 1)
                dve.wait_ge(small_hi_set, 1)
                dve.tensor_tensor(small_lo[:], small_t[:, 0:3, :], small_hi[:].bitcast(F32),
                                  ALU.subtract).then_inc(small_lo_set, 1)

            def lower_halves(i):
                dve.wait_ge(stage_in[i % 2], 16 * (i // 2 + 1))
                if i == Q_W:
                    dve.wait_ge(q_scale_set, 1)
                for c in range(DC):
                    dve.wait_ge(w_hi_set, 4 * i + c + 1)
                    dve.scalar_tensor_tensor(out=weight_lo(i, c), in0=stage[:, i % 2, c, :],
                                             scalar=q_scale[:, c:c + 1] if i == Q_W else 1.0,
                                             in1=weight_hi(i, c).bitcast(F32), op0=ALU.mult,
                                             op1=ALU.subtract).then_inc(w_lo_set[i], 1)

            def prepare_vecs():
                dve.wait_ge(vecs_in, 16 * 6)
                dve.tensor_scalar(q_scale[:], vecs[:, 0, :], SCALE, None, ALU.mult).then_inc(q_scale_set, 1)

            def prepare_q():
                lower_halves(Q_W)
                dve.wait_ge(q_bias_done, 1)
                dve.tensor_tensor(q_bias[:], bank[2][:, 0:DC], vecs[:, 2, :], ALU.add).then_inc(q_bias_set, 1)
                dve.wait_ge(q_bias_set, 1)
                dve.tensor_scalar(q_bias[:], q_bias[:], SCALE, None, ALU.mult).then_inc(q_bias_set, 1)
                dve.wait_ge(q_bias_set, 2)

            def lower(out, psum, hi, done):
                dve.tensor_tensor(out, psum, hi.bitcast(F32), ALU.subtract).then_inc(done, 1)

            def slot(s):
                e0, e1, e2, ahead = s, s + -1, s + -2, s + 1
                if e0.exists():
                    dve.wait_ge(ctxT_hi_set, e0.nth(1, 1))
                    lower(flat(ctxT_lo), bank[0][:], flat(ctxT_hi), ctxT_lo_set)
                    for i, b in enumerate((1, 3)):
                        dve.wait_ge(m_hi_set, e0.nth(2, i + 1))
                        dve.scalar_tensor_tensor(out=m_lo[:, i, :], in0=bank[b][:], scalar=bias0[:, i:i + 1],
                                                 in1=m_hi[:, i, :].bitcast(F32), op0=ALU.add,
                                                 op1=ALU.subtract).then_inc(m_lo_set, 1)
                if e1.exists():
                    dve.wait_ge(xnT_hi_set, e1.nth(1, 1))
                    lower(flat(xnT_lo), bank[4][:], flat(xnT_hi), xnT_lo_set)
                    dve.wait_ge(mask_loaded[e1.parity], e1.dma())
                    if e1.has_before(1):
                        dve.wait_ge(s1_done, (e1 + -1).nth(2, 2))
                    dve.tensor_scalar(mask_less_1[:], mask_u8[:, e1.parity, :], -1.0, None,
                                      ALU.add).then_inc(mask_set, 1)
                if ahead.exists():
                    u = ahead.parity
                    dve.wait_ge(x_loaded[u], ahead.dma())
                    dve.bn_stats(in_stats[:, 0, :], x_in[:, u, :]).then_inc(in_stat, 1)
                    dve.wait_ge(ctx_loaded[u], ahead.dma())
                    dve.bn_stats(in_stats[:, 1, :], ctx_in[:, u, :]).then_inc(in_stat, 1)
                    dve.wait_ge(in_stat, ahead.nth(2, 2))
                    dve.sem_inc(stats_seen, 1)
                    for i in range(2):
                        dve.bn_aggr(in_mv[:, i, :], in_stats[:, i, :]).then_inc(in_aggr, 1)
                    dve.wait_ge(in_aggr, ahead.nth(2, 2))
                    dve.tensor_scalar(in_ve[:], in_mv[:, :, 1], EPS, None, ALU.add).then_inc(in_veps, 1)
                if e2.exists():
                    dve.wait_ge(cproj_done, e2.nth(1, 1))
                    dve.wait_ge(x1b_set, e2.nth(1, 1))
                    if e2.has_before(2):
                        dve.wait_ge(hid_stored[e2.parity], (e2 + -2).dma())
                    dve.tensor_tensor(hid[:, e2.parity, :], bank[2][:], x1b[:, e2.parity, :],
                                      ALU.add).then_inc(hid_set, 1)

                def max0(t):
                    dve.wait_ge(s0_done, e0.nth(4, t + 1))
                    if t == 0 and e0.has_before(1):
                        dve.wait_ge(exp0_done, (e0 + -1).nth(4, 4))
                    dve.tensor_reduce(negmax0[:, t:t + 1], bank[S0_BANK[t]][:], AX_X, ALU.max,
                                      negate=True).then_inc(max0_set, 1)

                if e0.exists():
                    max0(0)
                if ahead.exists():
                    dve.wait_ge(in_rstd_ready, ahead.nth(1, 1))
                    if ahead.has_before(1):
                        dve.wait_ge(m_done, (ahead + -1).nth(2, 2))
                        dve.wait_ge(normed_lo_set, (ahead + -1).nth(2, 2))
                    for i, src in enumerate((x_in, ctx_in)):
                        dve.tensor_scalar(normed[:, i, :], src[:, ahead.parity, :], in_mv[:, i, 0:1],
                                          in_rstd[:, i:i + 1], ALU.subtract, ALU.mult).then_inc(normed_set, 1)
                    for i in range(2):
                        dve.wait_ge(normed_set, ahead.nth(2, i + 1))
                        dve.tensor_copy(normed_hi[:, i, :], normed[:, i, :]).then_inc(normed_hi_set, 1)
                if e0.exists():
                    max0(1)
                    max0(2)
                if e1.exists():
                    dve.wait_ge(qT_turned, e1.nth(1, 1))
                    dve.tensor_tensor(qT[:], by_chunk(3), q_bias[:].unsqueeze(2).to_broadcast([P, DC, P]),
                                      ALU.add).then_inc(qT_set, 1)
                if e0.exists():
                    max0(3)

                def max1(r):
                    if e1.exists():
                        dve.wait_ge(s1_done, e1.nth(2, r // 2 + 1))
                        dve.tensor_reduce(negmax1[:, r, :], by_chunk(S1_BANK[r]), AX_X, ALU.max,
                                          negate=True).then_inc(max1_set, 1)

                def sum1_reciprocal(r):
                    if e1.exists():
                        dve.wait_ge(exp1_done, e1.nth(16, 4 * r + 4))
                        dve.reciprocal(rsum1[:, r, :], sum1[:, r, :]).then_inc(rsum1_set, 1)

                if e0.exists():
                    dve.wait_ge(exp0_done, e0.nth(4, 4))
                    dve.reciprocal(rsum0[:], sum0[:]).then_inc(rsum0_set, 1)
                    dve.wait_ge(rsum0_set, e0.nth(1, 1))

                def scale_A(t):
                    if e0.exists():
                        dve.tensor_scalar(A[:, t, :], A[:, t, :], rsum0[:, t:t + 1], None,
                                          ALU.mult).then_inc(a_scaled, 1)

                def at_lower(j):
                    if e0.exists():
                        dve.wait_ge(at_hi_set, e0.nth(4, j + 1))
                        lower(at_lo[:, j, :], bank[AT_BANK[j]][:], at_hi[:, j, :], at_lo_set)

                for t in range(DC):
                    scale_A(t)
                max1(0)
                if e0.exists():
                    dve.wait_ge(k_done, e0.nth(1, 1))
                    dve.tensor_copy(k_sb[:], bank[7][:]).then_inc(k_copied, 1)
                max1(1)
                sum1_reciprocal(0)
                at_lower(0)
                at_lower(1)
                max1(2)
                sum1_reciprocal(1)
                at_lower(2)
                max1(3)
                at_lower(3)
                sum1_reciprocal(2)
                if e0.exists():
                    dve.wait_ge(v_done, e0.nth(1, 1))
                    if not e0.has_before(1):
                        dve.wait_ge(vecs_in, 16 * 6)
                    dve.tensor_tensor(v_sb[:, e0.parity, :], bank[0][:], v_bias[:], ALU.add).then_inc(v_set, 1)
                sum1_reciprocal(3)
                if e1.exists() and not e0.exists():
                    for t in range(TILES):
                        mlp.statistics(dve, Item(0, 0, 1), t)
                if e0.exists():
                    dve.wait_ge(u_hi_set, e0.nth(1, 1))
                    lower(u_lo[:], bank[7][:], u_hi[:], u_lo_set)
                    dve.wait_ge(kT_turned, e0.nth(1, 1))
                    dve.tensor_tensor(kT[:], by_chunk(0), vecs[:, 3, :].unsqueeze(2).to_broadcast([P, DC, P]),
                                      ALU.add).then_inc(kT_set, 1)
                if e0.exists():
                    dve.wait_ge(out0_done, e0.nth(1, 1))
                    if e0.has_before(1):
                        dve.wait_ge(x1b_set, (e0 + -1).nth(1, 1))
                    dve.scalar_tensor_tensor(out=x1[:], in0=bank[7][:], scalar=out0_bias[:, 0:1],
                                             in1=x_in[:, e0.parity, :], op0=ALU.add, op1=ALU.add)\
                       .then_inc(x1_set, 1)
                    dve.wait_ge(x1_set, e0.nth(1, 1))
                    dve.bn_stats(x1_stats[:], x1[:]).then_inc(x1_stat, 1)
                    dve.wait_ge(x1_stat, e0.nth(1, 1))
                    dve.sem_inc(stats_seen, 1)
                    dve.bn_aggr(x1_mv[:], x1_stats[:]).then_inc(x1_aggr, 1)
                    dve.wait_ge(x1_aggr, e0.nth(1, 1))
                    dve.tensor_scalar(x1_ve[:], x1_mv[:, 1:2], EPS, None, ALU.add).then_inc(x1_veps, 1)
                if e1.exists():
                    dve.wait_ge(outT_hi_set, e1.nth(1, 1))
                    lower(flat(outT_lo), bank[2][:], flat(outT_hi), outT_lo_set)
                if e0.exists():
                    dve.wait_ge(x1_rstd_ready, e0.nth(1, 1))
                    dve.tensor_scalar(x1n[:], x1[:], x1_mv[:, 0:1], x1_rstd[:, 0:1],
                                      ALU.subtract, ALU.mult).then_inc(x1n_set, 1)

            def first_group():
                dve.wait_ge(outT_done, B)
                for t in range(TILES):
                    mlp.normalise(dve, Item(0, 0, 1), t)
                for c in range(STAGE):
                    mlp.lower_half(dve, mlp.first_lo[:, 0, c, :], mlp.first_hi[:, 0, c, :], 0, c)

            slots(dve, slot, {0: lambda: (prepare_small(), lower_halves(K_W), prepare_vecs()),
                              1: prepare_q, LAST: first_group})

        @block.tensor
        def _(pe):
            def three_passes(out, a_hi, a_lo, b_hi, b_lo, first=True, last=True):
                pe.matmul(out, a_hi, b_lo, start=first, stop=False)
                pe.matmul(out, a_lo, b_hi, start=False, stop=False)
                return pe.matmul(out, a_hi, b_hi, start=False, stop=last)

            def prepare_small():
                pe.wait_ge(small_in, 16 * 8)
                pe.wait_ge(ident_set, 1)
                for n, i in enumerate((0, 1, 3)):
                    pe.transpose(bank[n][:, 0:P], small[:, i, :], ident[:]).then_inc(small_turned, 1)
                pe.wait_ge(small_copied, 3)
                pe.matmul(bank[3][:, 0:P], small[:, 2, :], small_t[:, 3, :], start=True, stop=True)\
                  .then_inc(wow_done, 1)
                pe.matmul(bank[4][:, 0:1], small_t[:, 3, :], bias0[:, 2:3], start=True, stop=True)\
                  .then_inc(wow_done, 1)
                pe.wait_ge(wow_copied, 2)
                pe.wait_ge(small_lo_set, 1)

            def prepare_q_bias():
                pe.wait_ge(vecs_in, 16 * 6)
                pe.wait_ge(stage_in[Q_W % 2], 32)
                for m in range(DC):
                    for c in range(DC):
                        last = pe.matmul(bank[2][:, m:m + 1], stage[:, Q_W % 2, c, m * P:(m + 1) * P],
                                         vecs[:, 1, c:c + 1], start=(c == 0), stop=(c == DC - 1))
                last.then_inc(q_bias_done, 1)

            def turn(out, src, done):
                for c in range(DC):
                    last = pe.transpose(out[:, c * P:(c + 1) * P], src(c), ident[:])
                last.then_inc(done, 1)

            def project(out, hi, lo, weight, done, chunks=range(DC)):
                for c in chunks:
                    last = three_passes(out[:], hi[:, c, :], lo[:, c, :], weight_hi(weight, c),
                                        weight_lo(weight, c), c == 0, c == DC - 1)
                if c == DC - 1:
                    last.then_inc(done, 1)

            def slot(s):
                e0, e1, e2 = s, s + -1, s + -2

                if e0.exists():
                    if e1.exists():
                        pe.wait_ge(kT_set, e1.nth(1, 1))
                    pe.wait_ge(ctx_loaded[e0.parity], e0.dma())
                    turn(bank[0], lambda c: ctx_in[:, e0.parity, c * P:(c + 1) * P], ctxT_turned)
                    for i, b in enumerate((1, 3)):
                        pe.wait_ge(normed_lo_set, e0.nth(2, i + 1))
                        three_passes(bank[b][:], small_hi[:, i, :], small_lo[:, i, :], normed_hi[:, i, :],
                                     normed_lo[:, i, :]).then_inc(m_done, 1)
                if e2.exists():
                    if not e2.has_before(1):
                        pe.wait_ge(w_lo_set[C_W], 4)
                    pe.wait_ge(outT_lo_set, e2.nth(1, 1))
                    project(bank[2], outT_hi, outT_lo, C_W, cproj_done, range(0, 2))
                if e1.exists():
                    pe.wait_ge(x1n_set, e1.nth(1, 1))
                    turn(bank[4], lambda c: x1n[:, c * P:(c + 1) * P], xnT_turned)
                if e2.exists():
                    project(bank[2], outT_hi, outT_lo, C_W, cproj_done, range(2, 4))

                def scores0(t):
                    if e0.exists():
                        if t == 0:
                            pe.wait_ge(m_lo_set, e0.nth(2, 2))
                        if t == 2:
                            pe.wait_ge(ctxT_lo_set, e0.nth(1, 1))
                        cols = slice(t * P, (t + 1) * P)
                        three_passes(bank[S0_BANK[t]][:], m_hi[:, 0, cols], m_lo[:, 0, cols], m_hi[:, 1, :],
                                     m_lo[:, 1, :]).then_inc(s0_done, 1)

                scores0(0)
                if e1.exists():
                    if not e1.has_before(1):
                        pe.wait_ge(w_lo_set[Q_W], 4)
                    pe.wait_ge(xnT_lo_set, e1.nth(1, 1))
                    project(bank[7], xnT_hi, xnT_lo, Q_W, q_done)
                scores0(1)
                scores0(2)
                scores0(3)
                if e1.exists():
                    pe.wait_ge(q_copied, e1.nth(1, 1))
                    turn(bank[3], lambda c: q_sb[:, c * P:(c + 1) * P], qT_turned)

                def scores1(pair):
                    rs = (2 * pair, 2 * pair + 1)
                    if pair == 0:
                        if e2.exists():
                            pe.wait_ge(hid_set, e2.nth(1, 1))
                        pe.wait_ge(mask_set, e1.nth(1, 1))
                        pe.wait_ge(kT_set, e1.nth(1, 1))
                        pe.wait_ge(qT_set, e1.nth(1, 1))
                    elif e0.exists():
                        pe.wait_ge(exp0_done, e0.nth(4, 2))
                    for r in rs:
                        row = slice(32 * r, 32 * r + 1)
                        pe.matmul(by_chunk(S1_BANK[r]), masked_bf[row, :],
                                  mask_less_1[row, :].unsqueeze(1).to_broadcast([1, 4, P]), start=True, stop=False)
                    for c in range(4):
                        for r in rs:
                            rows = slice(32 * r, 32 * r + 32)
                            mm = pe.matmul(bank[S1_BANK[r]][:, c * P:(c + 1) * P], qT[rows, c, :], kT[rows, c, :],
                                           start=False, stop=(c == 3))
                    mm.then_inc(s1_done, 1)

                def turn_A(j):
                    if e0.exists():
                        if j == 0:
                            pe.wait_ge(a_scaled, e0.nth(4, 4))
                        if j >= 2 and e1.exists():
                            pe.wait_ge(exp1_done, e1.nth(16, 4 * (j - 1)))
                        turn(bank[AT_BANK[j]], lambda t: A[:, t, j * P:(j + 1) * P], at_turned)

                def values0(j):
                    if e0.exists():
                        if j == 0:
                            pe.wait_ge(k_copied, e0.nth(1, 1))
                        pe.wait_ge(at_lo_set, e0.nth(4, j + 1))
                        last = three_passes(bank[7][:], ctxT_hi[:, j, :], ctxT_lo[:, j, :], at_hi[:, j, :],
                                            at_lo[:, j, :], j == 0, j == DC - 1)
                        if j == DC - 1:
                            last.then_inc(u_done, 1)

                def turn_probs(r):
                    if e1.exists():
                        pe.wait_ge(exp1_done, e1.nth(16, 4 * r + 4))
                        pe.wait_ge(probs_set, e1.nth(4, r + 1))
                        turn(bank[PT_BANK[r]], lambda c: probs[:, r, c, :], pT_turned)

                if e0.exists():
                    if not e0.has_before(1):
                        pe.wait_ge(w_lo_set[K_W], 4)
                    project(bank[7], ctxT_hi, ctxT_lo, K_W, k_done, range(0, 2))
                if e1.exists():
                    scores1(0)
                if e0.exists():
                    project(bank[7], ctxT_hi, ctxT_lo, K_W, k_done, range(2, 4))
                turn_A(0)
                if e0.exists():
                    if not e0.has_before(1):
                        pe.wait_ge(w_lo_set[V_W], 4)
                    pe.wait_ge(exp0_done, e0.nth(4, 3))
                    project(bank[0], ctxT_hi, ctxT_lo, V_W, v_done, range(0, 2))
                turn_A(1)
                if e1.exists():
                    scores1(1)
                turn_A(2)
                if e0.exists():
                    project(bank[0], ctxT_hi, ctxT_lo, V_W, v_done, range(2, 4))
                turn_A(3)
                values0(0)
                values0(1)
                values0(2)
                turn_probs(0)
                values0(3)
                turn_probs(1)
                turn_probs(2)
                if e0.exists():
                    pe.wait_ge(v_set, e0.nth(1, 1))
                    pe.wait_ge(k_copied, e0.nth(1, 1))
                    turn(bank[0], lambda c: k_sb[:, c * P:(c + 1) * P], kT_turned)
                turn_probs(3)
                if e0.exists():
                    pe.wait_ge(u_lo_set, e0.nth(1, 1))
                    three_passes(bank[7][:], small_hi[:, 2, :], small_lo[:, 2, :], u_hi[:], u_lo[:])\
                        .then_inc(out0_done, 1)
                if e1.exists():
                    pe.wait_ge(pT_copied, e1.nth(4, 4))
                    for c in range(4):
                        for r in range(4):
                            h = 4 * c + r
                            mm = pe.matmul(bank[2][32 * r:32 * r + 32, c * P:(c + 1) * P],
                                           v_sb[:, e1.parity, h * HD:(h + 1) * HD], pT[:, r, c, :],
                                           start=True, stop=True)
                    mm.then_inc(outT_done, 1)

            slots(pe, slot, {0: prepare_small, 1: prepare_q_bias})


def mlp_pass(nc, hidden, w, out, mlp):
    B, _, D = hidden.shape
    DC = D // P
    INNER = w["fc_w"].shape[1]
    IC = INNER // P
    N = TILES * P
    G = B // TILES
    STAGES = 2 * IC // STAGE
    assert B % TILES == 0 and DC == STAGE and IC % STAGE == 0

    with ExitStack() as stack:
        def sb(name, shape, dt=F32):
            return stack.enter_context(nc.sbuf_tensor(name, shape, dt))

        def sem(name):
            return stack.enter_context(nc.semaphore(name))

        acc = [stack.enter_context(nc.psum_tensor(f"acc{i}", [P, D], F32)) for i in range(TILES)]
        pre = [stack.enter_context(nc.psum_tensor(f"pre{i}", [P, N], F32)) for i in range(2)]
        tr = [stack.enter_context(nc.psum_tensor(f"tr{i}", [P, N], F32)) for i in range(2)]

        rest_hi = sb("rest_hi", [P, STAGES - 2, STAGE, 512], F32R)
        rest_lo = sb("rest_lo", [P, STAGES - 2, STAGE, 512], F32R)
        proj_bias = sb("proj_bias", [P, D])
        yT = sb("yT", [P, 2, N])
        yT_hi = sb("yT_hi", [P, DC, N], F32R)
        yT_lo = sb("yT_lo", [P, DC, N], F32R)
        gl = sb("gl", [P, 2, N])
        hT_hi = sb("hT_hi", [P, 2, N], F32R)
        hT_lo = sb("hT_lo", [P, 2, N], F32R)

        proj_bias_in = sem("proj_bias_in")
        out_stored = [sem(f"out_stored{i}") for i in range(2)]
        bias_added = sem("bias_added")
        yT_turned = sem("yT_turned")
        yT_set = sem("yT_set")
        yT_hi_set = sem("yT_hi_set")
        yT_lo_set = sem("yT_lo_set")
        fc_done = sem("fc_done")
        gelu_done = sem("gelu_done")
        hT_hi_set = sem("hT_hi_set")
        hT_lo_set = sem("hT_lo_set")
        proj_done = sem("proj_done")
        out_set = sem("out_set")

        PAIRS = (G - 2) // 2

        def groups(eng, group):
            group(Item(0, 0, G), True)
            with eng.Fori(0, PAIRS) as pair:
                for g in range(1, 3):
                    group(Item(pair, g, G), False)
            for g in range(1 + 2 * PAIRS, G):
                group(Item(0, g, G), False)

        ident, stage, rows, y = mlp.ident, mlp.stage, mlp.rows, mlp.y

        def weight_hi(n, c):
            return mlp.first_hi[:, n, c, :] if n < 2 else rest_hi[:, n - 2, c, :]

        def weight_lo(n, c):
            return mlp.first_lo[:, n, c, :] if n < 2 else rest_lo[:, n - 2, c, :]

        block = stack.enter_context(nc.Block())

        @block.sync
        def _(sp):
            sp.dma_start(proj_bias[:], w["proj_b"].partition_broadcast(P)).then_inc(proj_bias_in, 16)
            for u in range(2):
                sp.wait_ge(mlp.hid_stored[u], 16 * (B // 2))
            mlp.load_rows(sp, hidden, Item(0, 1, G))
            for n in range(2, STAGES):
                sp.wait_ge(mlp.w_hi_set, STAGE * (n - 1))
                sp.wait_ge(mlp.w_lo_set, STAGE * (n - 1))
                sp.dma_start(stage[:, n % 2, :, :], mlp_stage_source(w, n)).then_inc(mlp.staged[n % 2], 16)

            def group(g, first):
                if (g + 1).exists() and not first:
                    sp.wait_ge(out_stored[(g + 1).parity], (g + -1).dma(TILES))
                    mlp.load_rows(sp, hidden, g + 1)
                for t in range(TILES):
                    sp.wait_ge(out_set, g.nth(TILES, t + 1))
                    sp.dma_start(out[g.number * TILES + t], rows[:, g.parity, t, :])\
                      .then_inc(out_stored[g.parity], 16)

            groups(sp, group)
            for u in range(2):
                sp.wait_ge(out_stored[u], 16 * TILES * (G // 2))

        @block.gpsimd
        def _(pool):
            def add_bias(g):
                if not g.has_before(1):
                    pool.wait_ge(proj_bias_in, 16)
                for t in range(TILES):
                    pool.wait_ge(mlp.y_set, g.nth(4, t + 1))
                    pool.tensor_tensor(rows[:, g.parity, t, :], rows[:, g.parity, t, :], proj_bias[:],
                                       ALU.add).then_inc(bias_added, 1)

            add_bias(Item(0, 0, G))

            def group(g, first):
                if (g + 1).exists():
                    mlp.inverse_deviations(pool, g + 1)
                    add_bias(g + 1)

            groups(pool, group)

        @block.scalar
        def _(act):
            def turned(g, c):
                act.wait_ge(yT_turned, g.nth(4, c + 1))
                if c >= 2:
                    act.wait_ge(yT_lo_set, g.nth(4, c - 1))
                elif g.has_before(1):
                    act.wait_ge(yT_lo_set, (g + -1).nth(4, c + 3))
                act.activation(yT[:, c % 2, :], tr[c % 2][:], ACT.Identity, scale=mlp.ln_vecs[:, 0, c:c + 1],
                               bias=mlp.ln_vecs[:, 1, c:c + 1]).then_inc(yT_set, 1)

            act.wait_ge(mlp.vecs_in, 16 * 3)
            for c in range(DC):
                turned(Item(0, 0, G), c)

            def group(g, first):
                for i in range(IC):
                    act.wait_ge(fc_done, g.nth(IC, i + 1))
                    if i >= 2:
                        act.wait_ge(hT_lo_set, g.nth(IC, i - 1))
                    elif g.has_before(1):
                        act.wait_ge(hT_lo_set, (g + -1).nth(IC, IC - 1 + i))
                    act.activation(gl[:, i % 2, :], pre[i % 2][:], ACT.Gelu_apprx_tanh,
                                   bias=mlp.fc_bias[:, i:i + 1]).then_inc(gelu_done, 1)
                    if first and i < IC - STAGE:
                        for j in range(2 * i, 2 * i + 2):
                            n, c = 2 + j // STAGE, j % STAGE
                            mlp.upper_half(act, weight_hi(n, c), n, c)
                if (g + 1).exists():
                    for c in range(DC):
                        turned(g + 1, c)

            groups(act, group)

        @block.vector
        def _(dve):
            def turned(g, c):
                dve.wait_ge(yT_set, g.nth(4, c + 1))
                if c == 0 and g.has_before(1):
                    dve.wait_ge(fc_done, (g + -1).nth(IC, IC))
                dve.tensor_copy(yT_hi[:, c, :], yT[:, c % 2, :]).then_inc(yT_hi_set, 1)
                dve.wait_ge(yT_hi_set, g.nth(4, c + 1))
                dve.tensor_tensor(yT_lo[:, c, :], yT[:, c % 2, :], yT_hi[:, c, :].bitcast(F32),
                                  ALU.subtract).then_inc(yT_lo_set, 1)

            for c in range(DC):
                turned(Item(0, 0, G), c)

            def group(g, first):
                nxt = g + 1
                for i in range(IC):
                    dve.wait_ge(gelu_done, g.nth(IC, i + 1))
                    if i >= 2:
                        dve.wait_ge(proj_done, g.nth(IC, i - 1))
                    elif g.has_before(1):
                        dve.wait_ge(proj_done, (g + -1).nth(IC, IC - 1 + i))
                    dve.tensor_copy(hT_hi[:, i % 2, :], gl[:, i % 2, :]).then_inc(hT_hi_set, 1)
                    dve.wait_ge(hT_hi_set, g.nth(IC, i + 1))
                    dve.tensor_tensor(hT_lo[:, i % 2, :], gl[:, i % 2, :], hT_hi[:, i % 2, :].bitcast(F32),
                                      ALU.subtract).then_inc(hT_lo_set, 1)
                    if first and i < IC - STAGE:
                        for j in range(2 * i, 2 * i + 2):
                            n, c = 2 + j // STAGE, j % STAGE
                            mlp.lower_half(dve, weight_lo(n, c), weight_hi(n, c), n, c)
                    if nxt.exists():
                        if 5 <= i < 5 + TILES:
                            mlp.statistics(dve, nxt, i - 5)
                        if 10 <= i < 10 + TILES:
                            if i == 10:
                                dve.wait_ge(yT_turned, g.nth(4, 4))
                            mlp.normalise(dve, nxt, i - 10)
                if nxt.exists():
                    for c in range(DC):
                        turned(nxt, c)
                for t in range(TILES):
                    if t == 0:
                        dve.wait_ge(proj_done, g.nth(IC, IC))
                    dve.wait_ge(bias_added, g.nth(4, t + 1))
                    dve.tensor_tensor(rows[:, g.parity, t, :], acc[t][:], rows[:, g.parity, t, :],
                                      ALU.add).then_inc(out_set, 1)

            groups(dve, group)

        @block.tensor
        def _(pe):
            def turn(g, c):
                if c == 0:
                    pe.wait_ge(mlp.y_set, g.nth(4, 4))
                if c >= 2:
                    pe.wait_ge(yT_set, g.nth(4, c - 1))
                elif g.has_before(1):
                    pe.wait_ge(yT_set, (g + -1).nth(4, c + 3))
                for t in range(TILES):
                    last = pe.transpose(tr[c % 2][:, t * P:(t + 1) * P], y[:, t, c * P:(c + 1) * P], ident[:])
                last.then_inc(yT_turned, 1)

            def three_passes(out, a_hi, a_lo, b_hi, b_lo, first, last):
                pe.matmul(out, a_hi, b_lo, start=first, stop=False)
                pe.matmul(out, a_lo, b_hi, start=False, stop=False)
                return pe.matmul(out, a_hi, b_hi, start=False, stop=last)

            def fc(g, i):
                if i >= 2:
                    pe.wait_ge(gelu_done, g.nth(IC, i - 1))
                elif g.has_before(1):
                    pe.wait_ge(gelu_done, (g + -1).nth(IC, IC - 1 + i))
                n, cols = i // STAGE * 2, slice(i % STAGE * P, (i % STAGE + 1) * P)
                for c in range(DC):
                    if i == 0:
                        pe.wait_ge(yT_lo_set, g.nth(4, c + 1))
                    if not g.has_before(1) and i % STAGE == 0:
                        pe.wait_ge(mlp.w_lo_set, STAGE * n + c + 1)
                    last = three_passes(pre[i % 2][:], weight_hi(n, c)[:, cols], weight_lo(n, c)[:, cols],
                                        yT_hi[:, c, :], yT_lo[:, c, :], c == 0, c == DC - 1)
                last.then_inc(fc_done, 1)

            def proj(g, i):
                pe.wait_ge(hT_lo_set, g.nth(IC, i + 1))
                if not g.has_before(1):
                    pe.wait_ge(mlp.w_lo_set, STAGE * (i // STAGE * 2 + 1) + i % STAGE + 1)
                if i == 0 and g.has_before(1):
                    pe.wait_ge(out_set, (g + -1).nth(4, 4))
                n, c = i // STAGE * 2 + 1, i % STAGE
                for t in range(TILES):
                    cols = slice(t * P, (t + 1) * P)
                    last = three_passes(acc[t][:], hT_hi[:, i % 2, cols], hT_lo[:, i % 2, cols], weight_hi(n, c),
                                        weight_lo(n, c), i == 0, i == IC - 1)
                last.then_inc(proj_done, 1)

            for c in range(DC):
                turn(Item(0, 0, G), c)

            def group(g, first):
                more = (g + 1).exists()
                for i in range(IC):
                    fc(g, i)
                    if i == IC - 1 and more:
                        turn(g + 1, 0)
                        turn(g + 1, 1)
                    if i >= 1:
                        proj(g, i - 1)
                if more:
                    turn(g + 1, 2)
                    turn(g + 1, 3)
                proj(g, IC - 1)

            groups(pe, group)


def kernel(**inputs):
    import numpy as np
    import concourse.bacc as bacc
    from concourse.bass_utils import run_bass_kernel_spmd

    nc = bacc.Bacc("TRN2", target_bir_lowering=False, num_devices=1)
    arrays, aps = {}, {}
    for name, value in inputs.items():
        a = np.ascontiguousarray(value)
        if a.dtype == np.bool_:
            a = a.view(np.uint8)
        arrays[f"in_{name}"] = a
        aps[name] = nc.dram_tensor(f"in_{name}", a.shape, mybir.dt.from_np(a.dtype), kind="ExternalInput").ap()
    shape = inputs["x"].shape
    out = nc.dram_tensor("out", shape, F32, kind="ExternalOutput").ap()
    hidden = nc.dram_tensor("hidden", shape, F32, kind="Internal").ap()
    w = {name.split("_xattn_", 1)[1]: ap for name, ap in aps.items() if "_xattn_" in name}
    with ExitStack() as stack:
        mlp = Handover(nc, stack)
        attention_pass(nc, aps["x"], aps["ctx_2048"], aps["mask_BxS2_bf1"], w, hidden, mlp)
        mlp_pass(nc, hidden, w, out, mlp)
    r = run_bass_kernel_spmd(nc, [arrays], core_ids=[0])
    return r.results[0]["out"]
```
